# Optimizing a Trainium2 kernel written in Bass

```python
import numpy as np
import jax
import jax.numpy as jnp

def _softmax(x, axis=-1):
    return jax.nn.softmax(x, axis=axis)

def _gelu(x):
    return jax.nn.gelu(x, approximate=True)

def _silu(x):
    return jax.nn.silu(x)

def _sigmoid(x):
    return jax.nn.sigmoid(x)

def _layernorm(x, axis=-1, eps=1e-05):
    m = jnp.mean(x, axis=axis, keepdims=True)
    v = jnp.var(x, axis=axis, keepdims=True)
    return (x - m) / jnp.sqrt(v + eps)

def _scatter_add(tgt, idx, src, axis=0):
    return tgt.at[idx].add(src)

def _segment_sum(src, seg, n):
    return jax.ops.segment_sum(src, seg, n)
kernel_name = 'mk_sandwich_d1_jaxref_r4_9a8496'

def setup_inputs(seed: int=0):
    np.random.seed(seed)
    _w = jnp.asarray

    def _L0_attn_setup():
        import jax, jax.numpy as jnp
        import numpy as np
        D_MODEL = 256
        D_STATE = 16
        EXPAND = 2
        D_CONV = 4
        D_INNER = D_MODEL * EXPAND
        DT_RANK = 64
        BATCH = 2
        SEQLEN = 512

        def _causal_conv_silu(x, w, b):
            K = w.shape[-1]
            xc = jnp.transpose(x, (0, 2, 1))
            xc = jnp.pad(xc, ((0, 0), (0, 0), (K - 1, 0)))
            y = jax.lax.conv_general_dilated(xc, w, (1,), 'VALID', dimension_numbers=('NCH', 'OIH', 'NCH'), feature_group_count=w.shape[0])
            y = y + b[None, :, None]
            return jax.nn.silu(jnp.transpose(y, (0, 2, 1)))

        def _ssm_scan(x, dt, A, Bm, Cm, D, z):

            def step(h, inp):
                x_t, dt_t, B_t, C_t = inp
                dA = jnp.exp(dt_t[:, :, None] * A[None])
                h = dA * h + (dt_t * x_t)[:, :, None] * B_t[:, None, :]
                y = jnp.einsum('bdn,bn->bd', h, C_t) + D * x_t
                return (h, y)
            Bz, L, Di = x.shape
            h0 = jnp.zeros((Bz, Di, A.shape[1]), x.dtype)
            xs = (x.swapaxes(0, 1), dt.swapaxes(0, 1), Bm.swapaxes(0, 1), Cm.swapaxes(0, 1))
            _, ys = jax.lax.scan(step, h0, xs)
            return ys.swapaxes(0, 1) * jax.nn.silu(z)

        def _branch(x_in, z, conv_w, conv_b, xp_w, dt_w, dt_b, A_log, Dp):
            xc = _causal_conv_silu(x_in, conv_w, conv_b)
            proj = xc @ xp_w.T
            dt, Bm, Cm = jnp.split(proj, [DT_RANK, DT_RANK + D_STATE], axis=-1)
            dt = jax.nn.softplus(dt @ dt_w.T + dt_b)
            return _ssm_scan(xc, dt, -jnp.exp(A_log), Bm, Cm, Dp, z)
        key = jax.random.key(seed)
        ks = jax.random.split(key, 16)
        s = 0.02
        inp = {'u': jax.random.normal(ks[0], (BATCH, SEQLEN, D_MODEL), jnp.float32), 'in_proj_w': jax.random.normal(ks[1], (2 * D_INNER, D_MODEL), jnp.float32) * s, 'out_proj_w': jax.random.normal(ks[2], (D_MODEL, D_INNER), jnp.float32) * s, 'fwd_conv_w': jax.random.normal(ks[3], (D_INNER, 1, D_CONV), jnp.float32) * 0.1, 'fwd_conv_b': jax.random.normal(ks[4], (D_INNER,), jnp.float32) * 0.01, 'fwd_x_proj_w': jax.random.normal(ks[5], (DT_RANK + 2 * D_STATE, D_INNER), jnp.float32) * s, 'fwd_dt_w': jax.random.normal(ks[6], (D_INNER, DT_RANK), jnp.float32) * s, 'fwd_dt_b': jax.random.normal(ks[7], (D_INNER,), jnp.float32) * 0.01, 'fwd_A_log': jnp.tile(jnp.log(jnp.arange(1, D_STATE + 1, dtype=jnp.float32)), (D_INNER, 1)), 'fwd_D': jnp.ones((D_INNER,), jnp.float32), 'bwd_conv_w': jax.random.normal(ks[8], (D_INNER, 1, D_CONV), jnp.float32) * 0.1, 'bwd_conv_b': jax.random.normal(ks[9], (D_INNER,), jnp.float32) * 0.01, 'bwd_x_proj_w': jax.random.normal(ks[10], (DT_RANK + 2 * D_STATE, D_INNER), jnp.float32) * s, 'bwd_dt_w': jax.random.normal(ks[11], (D_INNER, DT_RANK), jnp.float32) * s, 'bwd_dt_b': jax.random.normal(ks[12], (D_INNER,), jnp.float32) * 0.01, 'bwd_A_log': jnp.tile(jnp.log(jnp.arange(1, D_STATE + 1, dtype=jnp.float32)), (D_INNER, 1)), 'bwd_D': jnp.ones((D_INNER,), jnp.float32)}
        return inp
    _L0_attn_in = _L0_attn_setup()

    def _L0_ffn_setup():
        import jax, jax.numpy as jnp
        import numpy as np
        import math
        B, T, D, H, E, TOPK, CAPF = (4, 512, 256, 16, 8, 2, 2.0)
        HD = D // H

        def layernorm(x, g, b, eps=1e-05):
            m = jnp.mean(x, -1, keepdims=True)
            v = jnp.mean(jnp.square(x - m), -1, keepdims=True)
            return (x - m) * jax.lax.rsqrt(v + eps) * g + b

        def block_forward(x, ln1_g, ln1_b, Wqkv, Wproj, ln2_g, ln2_b, Wgate, W1, b1, W2, b2):
            Bb, Tt, d = x.shape
            hd = HD
            half = hd // 2
            h = layernorm(x, ln1_g, ln1_b)
            qkv = (h @ Wqkv).reshape(Bb, Tt, H, 3 * hd)
            q, k, v = (qkv[..., :hd], qkv[..., hd:2 * hd], qkv[..., 2 * hd:])
            inv_freq = 1.0 / 10000.0 ** (jnp.arange(0, hd, 2, dtype=jnp.float32) / hd)
            ang = jnp.arange(Tt, dtype=jnp.float32)[:, None] * inv_freq
            sin = jnp.sin(ang)[None, :, None, :].astype(x.dtype)
            cos = jnp.cos(ang)[None, :, None, :].astype(x.dtype)

            def rope(t):
                t1, t2 = (t[..., :half], t[..., half:])
                return jnp.concatenate([t1 * cos - t2 * sin, t1 * sin + t2 * cos], -1)
            q, k = (rope(q), rope(k))
            scores = jnp.einsum('bqhd,bkhd->bhqk', q, k) / math.sqrt(hd)
            causal = jnp.tril(jnp.ones((Tt, Tt), dtype=bool))
            scores = jnp.where(causal, scores, jnp.asarray(-1000000000.0, scores.dtype))
            probs = jax.nn.softmax(scores, axis=-1)
            attn = jnp.einsum('bhqk,bkhd->bqhd', probs, v).reshape(Bb, Tt, d) @ Wproj
            x = x + attn
            h2 = layernorm(x, ln2_g, ln2_b)
            flat = h2.reshape(-1, d)
            N = flat.shape[0]
            capacity = int(math.ceil(CAPF * N / E))
            gates = jax.nn.softmax((flat @ Wgate).astype(jnp.float32), -1).astype(flat.dtype)
            _, top_inds = jax.lax.top_k(gates, TOPK)
            mask = jnp.zeros((N, E), dtype=bool).at[jnp.arange(N)[:, None], top_inds].set(True)
            pos = jnp.cumsum(mask.astype(jnp.int32), axis=0) * mask - 1
            keep = (pos < capacity) & mask
            t_flat = jnp.repeat(jnp.arange(N), TOPK)
            e_flat = top_inds.reshape(-1)
            p = pos[t_flat, e_flat]
            kp = keep[t_flat, e_flat]
            p_eff = jnp.where(kp, p, capacity)
            exp_in = jnp.zeros((E, capacity, d), flat.dtype).at[e_flat, p_eff].set(flat[t_flat], mode='drop')
            hmid = jax.nn.gelu(jnp.einsum('ecd,edf->ecf', exp_in, W1) + b1[:, None, :], approximate=False)
            exp_out = jnp.einsum('ecf,efd->ecd', hmid, W2) + b2[:, None, :]
            gate = gates[t_flat, e_flat] * kp.astype(flat.dtype)
            p_g = jnp.minimum(p_eff, capacity - 1)
            moe = jnp.zeros((N, d), flat.dtype).at[t_flat].add(exp_out[e_flat, p_g] * gate[:, None])
            return x + moe.reshape(Bb, Tt, d)
        key = jax.random.key(seed)
        ks = jax.random.split(key, 8)
        s = 0.02
        return {'x': jax.random.normal(ks[0], (B, T, D), jnp.float32), 'ln1_g': jnp.ones((D,), jnp.float32), 'ln1_b': jnp.zeros((D,), jnp.float32), 'Wqkv': jax.random.normal(ks[1], (D, 3 * D), jnp.float32) * s, 'Wproj': jax.random.normal(ks[2], (D, D), jnp.float32) * s, 'ln2_g': jnp.ones((D,), jnp.float32), 'ln2_b': jnp.zeros((D,), jnp.float32), 'Wgate': jax.random.normal(ks[3], (D, E), jnp.float32) * s, 'W1': jax.random.normal(ks[4], (E, D, 4 * D), jnp.float32) * s, 'b1': jnp.zeros((E, 4 * D), jnp.float32), 'W2': jax.random.normal(ks[5], (E, 4 * D, D), jnp.float32) * s, 'b2': jnp.zeros((E, D), jnp.float32)}
    _L0_ffn_in = _L0_ffn_setup()
    _d = {'L0_attn_u': _L0_attn_in['u'], 'L0_attn_in_proj_w': _L0_attn_in['in_proj_w'], 'L0_attn_out_proj_w': _L0_attn_in['out_proj_w'], 'L0_attn_fwd_conv_w': _L0_attn_in['fwd_conv_w'], 'L0_attn_fwd_conv_b': _L0_attn_in['fwd_conv_b'], 'L0_attn_fwd_x_proj_w': _L0_attn_in['fwd_x_proj_w'], 'L0_attn_fwd_dt_w': _L0_attn_in['fwd_dt_w'], 'L0_attn_fwd_dt_b': _L0_attn_in['fwd_dt_b'], 'L0_attn_fwd_A_log': _L0_attn_in['fwd_A_log'], 'L0_attn_fwd_D': _L0_attn_in['fwd_D'], 'L0_attn_bwd_conv_w': _L0_attn_in['bwd_conv_w'], 'L0_attn_bwd_conv_b': _L0_attn_in['bwd_conv_b'], 'L0_attn_bwd_x_proj_w': _L0_attn_in['bwd_x_proj_w'], 'L0_attn_bwd_dt_w': _L0_attn_in['bwd_dt_w'], 'L0_attn_bwd_dt_b': _L0_attn_in['bwd_dt_b'], 'L0_attn_bwd_A_log': _L0_attn_in['bwd_A_log'], 'L0_attn_bwd_D': _L0_attn_in['bwd_D'], 'L0_ffn_ln1_g': _L0_ffn_in['ln1_g'], 'L0_ffn_ln1_b': _L0_ffn_in['ln1_b'], 'L0_ffn_Wqkv': _L0_ffn_in['Wqkv'], 'L0_ffn_Wproj': _L0_ffn_in['Wproj'], 'L0_ffn_ln2_g': _L0_ffn_in['ln2_g'], 'L0_ffn_ln2_b': _L0_ffn_in['ln2_b'], 'L0_ffn_Wgate': _L0_ffn_in['Wgate'], 'L0_ffn_W1': _L0_ffn_in['W1'], 'L0_ffn_b1': _L0_ffn_in['b1'], 'L0_ffn_W2': _L0_ffn_in['W2'], 'L0_ffn_b2': _L0_ffn_in['b2']}
    _x0 = _d['L0_attn_u']
    _d['L0_attn_u'] = jax.random.normal(jax.random.fold_in(jax.random.key(seed), 1), (2, 2048, 256), dtype=_x0.dtype)
    del _x0
    return _d

def reference(L0_attn_u, L0_attn_in_proj_w, L0_attn_out_proj_w, L0_attn_fwd_conv_w, L0_attn_fwd_conv_b, L0_attn_fwd_x_proj_w, L0_attn_fwd_dt_w, L0_attn_fwd_dt_b, L0_attn_fwd_A_log, L0_attn_fwd_D, L0_attn_bwd_conv_w, L0_attn_bwd_conv_b, L0_attn_bwd_x_proj_w, L0_attn_bwd_dt_w, L0_attn_bwd_dt_b, L0_attn_bwd_A_log, L0_attn_bwd_D, L0_ffn_ln1_g, L0_ffn_ln1_b, L0_ffn_Wqkv, L0_ffn_Wproj, L0_ffn_ln2_g, L0_ffn_ln2_b, L0_ffn_Wgate, L0_ffn_W1, L0_ffn_b1, L0_ffn_W2, L0_ffn_b2):

    def _L0_attn_ref(u, in_proj_w, out_proj_w, fwd_conv_w, fwd_conv_b, fwd_x_proj_w, fwd_dt_w, fwd_dt_b, fwd_A_log, fwd_D, bwd_conv_w, bwd_conv_b, bwd_x_proj_w, bwd_dt_w, bwd_dt_b, bwd_A_log, bwd_D):
        import jax, jax.numpy as jnp
        import numpy as np
        D_MODEL = 256
        D_STATE = 16
        EXPAND = 2
        D_CONV = 4
        D_INNER = D_MODEL * EXPAND
        DT_RANK = 64
        BATCH = 2
        SEQLEN = 512

        def _causal_conv_silu(x, w, b):
            K = w.shape[-1]
            xc = jnp.transpose(x, (0, 2, 1))
            xc = jnp.pad(xc, ((0, 0), (0, 0), (K - 1, 0)))
            y = jax.lax.conv_general_dilated(xc, w, (1,), 'VALID', dimension_numbers=('NCH', 'OIH', 'NCH'), feature_group_count=w.shape[0])
            y = y + b[None, :, None]
            return jax.nn.silu(jnp.transpose(y, (0, 2, 1)))

        def _ssm_scan(x, dt, A, Bm, Cm, D, z):

            def step(h, inp):
                x_t, dt_t, B_t, C_t = inp
                dA = jnp.exp(dt_t[:, :, None] * A[None])
                h = dA * h + (dt_t * x_t)[:, :, None] * B_t[:, None, :]
                y = jnp.einsum('bdn,bn->bd', h, C_t) + D * x_t
                return (h, y)
            Bz, L, Di = x.shape
            h0 = jnp.zeros((Bz, Di, A.shape[1]), x.dtype)
            xs = (x.swapaxes(0, 1), dt.swapaxes(0, 1), Bm.swapaxes(0, 1), Cm.swapaxes(0, 1))
            _, ys = jax.lax.scan(step, h0, xs)
            return ys.swapaxes(0, 1) * jax.nn.silu(z)

        def _branch(x_in, z, conv_w, conv_b, xp_w, dt_w, dt_b, A_log, Dp):
            xc = _causal_conv_silu(x_in, conv_w, conv_b)
            proj = xc @ xp_w.T
            dt, Bm, Cm = jnp.split(proj, [DT_RANK, DT_RANK + D_STATE], axis=-1)
            dt = jax.nn.softplus(dt @ dt_w.T + dt_b)
            return _ssm_scan(xc, dt, -jnp.exp(A_log), Bm, Cm, Dp, z)
        xz = u @ in_proj_w.T
        x_in, z = jnp.split(xz, 2, axis=-1)
        y_fwd = _branch(x_in, z, fwd_conv_w, fwd_conv_b, fwd_x_proj_w, fwd_dt_w, fwd_dt_b, fwd_A_log, fwd_D)
        x_flip, z_flip = (x_in[:, ::-1, :], z[:, ::-1, :])
        y_bwd = _branch(x_flip, z_flip, bwd_conv_w, bwd_conv_b, bwd_x_proj_w, bwd_dt_w, bwd_dt_b, bwd_A_log, bwd_D)[:, ::-1, :]
        return (y_fwd + y_bwd) @ out_proj_w.T

    def _L0_ffn_ref(x, ln1_g, ln1_b, Wqkv, Wproj, ln2_g, ln2_b, Wgate, W1, b1, W2, b2):
        import jax, jax.numpy as jnp
        import numpy as np
        import math
        B, T, D, H, E, TOPK, CAPF = (4, 512, 256, 16, 8, 2, 2.0)
        HD = D // H

        def layernorm(x, g, b, eps=1e-05):
            m = jnp.mean(x, -1, keepdims=True)
            v = jnp.mean(jnp.square(x - m), -1, keepdims=True)
            return (x - m) * jax.lax.rsqrt(v + eps) * g + b

        def block_forward(x, ln1_g, ln1_b, Wqkv, Wproj, ln2_g, ln2_b, Wgate, W1, b1, W2, b2):
            Bb, Tt, d = x.shape
            hd = HD
            half = hd // 2
            h = layernorm(x, ln1_g, ln1_b)
            qkv = (h @ Wqkv).reshape(Bb, Tt, H, 3 * hd)
            q, k, v = (qkv[..., :hd], qkv[..., hd:2 * hd], qkv[..., 2 * hd:])
            inv_freq = 1.0 / 10000.0 ** (jnp.arange(0, hd, 2, dtype=jnp.float32) / hd)
            ang = jnp.arange(Tt, dtype=jnp.float32)[:, None] * inv_freq
            sin = jnp.sin(ang)[None, :, None, :].astype(x.dtype)
            cos = jnp.cos(ang)[None, :, None, :].astype(x.dtype)

            def rope(t):
                t1, t2 = (t[..., :half], t[..., half:])
                return jnp.concatenate([t1 * cos - t2 * sin, t1 * sin + t2 * cos], -1)
            q, k = (rope(q), rope(k))
            scores = jnp.einsum('bqhd,bkhd->bhqk', q, k) / math.sqrt(hd)
            causal = jnp.tril(jnp.ones((Tt, Tt), dtype=bool))
            scores = jnp.where(causal, scores, jnp.asarray(-1000000000.0, scores.dtype))
            probs = jax.nn.softmax(scores, axis=-1)
            attn = jnp.einsum('bhqk,bkhd->bqhd', probs, v).reshape(Bb, Tt, d) @ Wproj
            x = x + attn
            h2 = layernorm(x, ln2_g, ln2_b)
            flat = h2.reshape(-1, d)
            N = flat.shape[0]
            capacity = int(math.ceil(CAPF * N / E))
            gates = jax.nn.softmax((flat @ Wgate).astype(jnp.float32), -1).astype(flat.dtype)
            _, top_inds = jax.lax.top_k(gates, TOPK)
            mask = jnp.zeros((N, E), dtype=bool).at[jnp.arange(N)[:, None], top_inds].set(True)
            pos = jnp.cumsum(mask.astype(jnp.int32), axis=0) * mask - 1
            keep = (pos < capacity) & mask
            t_flat = jnp.repeat(jnp.arange(N), TOPK)
            e_flat = top_inds.reshape(-1)
            p = pos[t_flat, e_flat]
            kp = keep[t_flat, e_flat]
            p_eff = jnp.where(kp, p, capacity)
            exp_in = jnp.zeros((E, capacity, d), flat.dtype).at[e_flat, p_eff].set(flat[t_flat], mode='drop')
            hmid = jax.nn.gelu(jnp.einsum('ecd,edf->ecf', exp_in, W1) + b1[:, None, :], approximate=False)
            exp_out = jnp.einsum('ecf,efd->ecd', hmid, W2) + b2[:, None, :]
            gate = gates[t_flat, e_flat] * kp.astype(flat.dtype)
            p_g = jnp.minimum(p_eff, capacity - 1)
            moe = jnp.zeros((N, d), flat.dtype).at[t_flat].add(exp_out[e_flat, p_g] * gate[:, None])
            return x + moe.reshape(Bb, Tt, d)
        return block_forward(x, ln1_g, ln1_b, Wqkv, Wproj, ln2_g, ln2_b, Wgate, W1, b1, W2, b2)
    x = L0_attn_u
    x = x + _layernorm(_L0_attn_ref(_layernorm(x, axis=-1), L0_attn_in_proj_w, L0_attn_out_proj_w, L0_attn_fwd_conv_w, L0_attn_fwd_conv_b, L0_attn_fwd_x_proj_w, L0_attn_fwd_dt_w, L0_attn_fwd_dt_b, L0_attn_fwd_A_log, L0_attn_fwd_D, L0_attn_bwd_conv_w, L0_attn_bwd_conv_b, L0_attn_bwd_x_proj_w, L0_attn_bwd_dt_w, L0_attn_bwd_dt_b, L0_attn_bwd_A_log, L0_attn_bwd_D), axis=-1)
    x = x + _layernorm(_L0_ffn_ref(_layernorm(x, axis=-1), L0_ffn_ln1_g, L0_ffn_ln1_b, L0_ffn_Wqkv, L0_ffn_Wproj, L0_ffn_ln2_g, L0_ffn_ln2_b, L0_ffn_Wgate, L0_ffn_W1, L0_ffn_b1, L0_ffn_W2, L0_ffn_b2), axis=-1)
    return x

_drawn_inputs = setup_inputs


def setup_inputs(seed=0):
    import zlib

    import numpy as np

    out = dict(_drawn_inputs(seed))
    spreads = {'L0_attn_fwd_D': (1.0, 0.2),
     'L0_attn_bwd_D': (1.0, 0.2),
     'L0_ffn_ln1_g': (1.0, 0.6),
     'L0_ffn_ln1_b': (0.0, 0.8),
     'L0_ffn_ln2_g': (1.0, 0.6),
     'L0_ffn_ln2_b': (0.0, 0.8),
     'L0_ffn_b1': (0.0, 0.8),
     'L0_ffn_b2': (0.0, 2.0)}
    factors = {'L0_attn_fwd_x_proj_w': 8.0,
     'L0_attn_fwd_dt_w': 45.489,
     'L0_attn_fwd_dt_b': 64.0,
     'L0_attn_fwd_A_log': 47.231,
     'L0_attn_bwd_x_proj_w': 8.0,
     'L0_attn_bwd_dt_w': 57.508,
     'L0_attn_bwd_dt_b': 64.0,
     'L0_attn_bwd_A_log': 48.282,
     'L0_ffn_Wqkv': 8.0,
     'L0_ffn_Wproj': 8.0,
     'L0_ffn_Wgate': 3.843,
     'L0_ffn_W1': 4.654,
     'L0_ffn_W2': 4.337}
    for name, (base, spread) in spreads.items():
        noise = np.random.default_rng([zlib.crc32(name.encode()), seed]).standard_normal(out[name].shape)
        drawn = base * np.exp(spread * noise) if base else spread * noise
        out[name] = jnp.asarray(drawn.astype(out[name].dtype))
    for name, factor in factors.items():
        out[name] = (out[name] * factor).astype(out[name].dtype)
    return out
```

```python
from contextlib import ExitStack

import concourse.bass as bass
from concourse import mybir

ACT = mybir.ActivationFunctionType
ALU = mybir.AluOpType
AX_X = mybir.AxisListType.X
F32 = mybir.dt.float32
BF16 = mybir.dt.bfloat16
I32 = mybir.dt.int32
U32 = mybir.dt.uint32

P = 128
B, L, D = 2, 2048, 256
NTOK = B * L
DI = 512
DT = DI // P
NS = 16
TAPS = 4
HALO = TAPS - 1
RANK = 64
C = 512
NC = L // C
JT = C // P
KD = D // P
H, HD = 16, 16
E, CAP, FF = 8, 1024, 1024
EPS = 1e-5
MASKED = -1e30
STACK = 6 * HD
BIG_SLOT = float(2 * E * CAP)


EXP_AND_LN = "natural_log_exp_and_others"


class Stage:

    def __init__(self, nc, name):
        self.nc, self.name = nc, name
        self.memory, self.program, self.used = ExitStack(), ExitStack(), []

    def __enter__(self):
        self.memory.__enter__()
        self.program.__enter__()
        return self

    def __exit__(self, *a):
        self.program.__exit__(*a)
        with self.nc.Block() as block:
            @block.gpsimd
            def _(pool):
                for sem in self.used:
                    pool.sem_clear(sem)
        return self.memory.__exit__(*a)

    def sb(self, name, shape, dt=F32):
        return self.memory.enter_context(self.nc.sbuf_tensor(f"{self.name}_{name}", shape, dt))

    def ps(self, name, shape, dt=F32):
        return self.memory.enter_context(self.nc.psum_tensor(f"{self.name}_{name}", shape, dt))

    def sems(self, *names):
        made = [self.memory.enter_context(self.nc.semaphore(f"{self.name}_{n}")) for n in names]
        self.used += made
        return made

    def pool_dma_sems(self, *names):
        return [self.nc.alloc_semaphore(f"{self.name}_{n}") for n in names]

    def block(self):
        return self.program.enter_context(self.nc.Block())


def make_constants(nc, st):
    k = {
        "ident": st.sb("ident", [P, P]),
        "identb": st.sb("identb", [P, P], BF16),
        "mask_qk": st.sb("mask_qk", [P, P], BF16),
        "mask_kq": st.sb("mask_kq", [P, P], BF16),
        "eps": st.sb("eps", [P, 1]),
        "one": st.sb("one", [P, 1]),
        "offsets": [st.sb(f"offsets{i}", [P, JT, 2], I32) for i in range(2)],
        "passed": st.sems("passed")[0],
    }
    with Stage(nc, "const") as s:
        (filled, shaped) = s.sems("filled", "shaped")
        block = s.block()

        @block.gpsimd
        def _(pool):
            pool.memset(k["ident"][:, :], 0.0).then_inc(filled, 1)
            pool.memset(k["identb"][:, :], 0.0).then_inc(filled, 1)
            pool.memset(k["mask_qk"][:, :], 0.0).then_inc(filled, 1)
            pool.memset(k["mask_kq"][:, :], 0.0).then_inc(filled, 1)
            pool.memset(k["eps"][:, :], EPS).then_inc(filled, 1)
            pool.memset(k["one"][:, :], 1.0).then_inc(filled, 1)
            pool.wait_ge(filled, 6)
            for name in ("ident", "identb"):
                pool.affine_select(out=k[name][:, :], in_=k[name][:, :], compare_op=ALU.not_equal, fill=1.0,
                                   base=0, pattern=[[-1, P]], channel_multiplier=1).then_inc(shaped, 1)
            pool.affine_select(out=k["mask_qk"][:, :], in_=k["mask_qk"][:, :], compare_op=ALU.is_ge, fill=MASKED,
                               base=0, pattern=[[-1, P]], channel_multiplier=1).then_inc(shaped, 1)
            pool.affine_select(out=k["mask_kq"][:, :], in_=k["mask_kq"][:, :], compare_op=ALU.is_ge, fill=MASKED,
                               base=0, pattern=[[1, P]], channel_multiplier=-1).then_inc(shaped, 1)
            pool.wait_ge(shaped, 4)
    return k


def hold(eng, k):
    eng.sem_inc(k["passed"], 1)


def ch_view(ap):
    return ap.rearrange("b (m p) l -> b p m l", p=P)


def tok_view(ap):
    return ap.rearrange("(b c j p) d -> b c p j d", b=B, c=NC, p=P)



def project_inputs(nc, k, u, in_wT, xin, sz, exp_in):
    with Stage(nc, "proj") as s:
        xt = [s.sb(f"xt{i}", [P, JT, D]) for i in range(2)]
        stats = s.sb("stats", [P, JT, 6])
        mv = s.sb("mv", [P, JT, 2])
        rstd = s.sb("rstd", [P, JT])
        xn = s.sb("xn", [P, JT, D])
        hT = [s.sb(f"hT{i}", [P, KD, C]) for i in range(2)]
        CLEARED = E * CAP * D // (B * NC * P)
        cleared = s.sb("cleared", [P, CLEARED])
        w = s.sb("w", [P, KD, 2 * DI])
        out_x = [s.sb(f"out_x{i}", [P, DT, C]) for i in range(2)]
        out_z = [s.sb(f"out_z{i}", [P, JT, DI]) for i in range(2)]
        zeros = s.sb("zeros", [P, DT, HALO])
        turn = [s.ps(f"turn{i}", [P, C]) for i in range(KD)]
        mmx = [s.ps(f"mmx{i}", [P, C]) for i in range(2)]
        mmz = [s.ps(f"mmz{i}", [P, C]) for i in range(2)]
        loaded_x = s.pool_dma_sems("loaded_x0", "loaded_x1")
        stored_x = s.sems("stored_x0", "stored_x1")
        stored_z = s.sems("stored_z0", "stored_z1")
        (loaded_w, stats_done, mv_done, log_done, rstd_done, xn_done, turned, h_act, h_dve,
         x_mm, z_mm, x_out, z_out, zeroed, pads, clears) = s.sems(
            "loaded_w", "stats_done", "mv_done", "log_done", "rstd_done", "xn_done", "turned",
            "h_act", "h_dve", "x_mm", "z_mm", "x_out", "z_out", "zeroed", "pads", "clears")
        slots_view = exp_in.rearrange("(t p r) d -> t p (r d)", t=B * NC, p=P)
        xview, xinv, szv = tok_view(u), ch_view(xin), tok_view(sz)
        block = s.block()

        @block.sync
        def _(sp):
            sp.dma_start(w[:, :, :], in_wT.rearrange("(k p) m -> p k m", p=P)).then_inc(loaded_w, 16)
            sp.wait_ge(zeroed, 2)
            for b in range(B):
                sp.dma_start(xinv[b, :, :, 0:HALO], zeros[:, :, :]).then_inc(pads, 16)
                sp.dma_start(xinv[b, :, :, HALO + L:], zeros[:, :, :]).then_inc(pads, 16)
            with sp.Fori(0, B) as b:
                for c in range(NC):
                    t = b * NC + c
                    sp.wait_ge(x_out, t * DT + DT + 2 * DT)
                    sp.dma_start(xinv[b, :, :, HALO + c * C:HALO + c * C + C], out_x[c % 2][:, :, :]
                                 ).then_inc(stored_x[c % 2], 16)
                    sp.wait_ge(z_out, t * DT + DT + 2 * DT)
                    sp.dma_start(szv[b, c], out_z[c % 2][:, :, :]).then_inc(stored_z[c % 2], 16)
                    sp.dma_start(slots_view[t], cleared[:, :]).then_inc(clears, 16)
            sp.wait_ge(pads, 16 * 2 * B)
            sp.wait_ge(clears, 16 * B * NC)
            for i in range(2):
                sp.wait_ge(stored_x[i], 16 * (B * NC // 2 + 1))
                sp.wait_ge(stored_z[i], 16 * (B * NC // 2 + 1))

        @block.gpsimd
        def _(pool):
            pool.memset(zeros[:, :, :], 0.0).then_inc(zeroed, 1)
            pool.memset(cleared[:, :], 0.0).then_inc(zeroed, 1)
            with pool.Fori(0, B) as b:
                for c in range(NC):
                    t = b * NC + c
                    pool.wait_ge(xn_done, t + 1)
                    hold(pool, k)
                    pool.dma_start(xt[c % 2][:, :, :], xview[b, c]).then_inc(loaded_x[c % 2], 16)
            pool.wait_ge(xn_done, B * NC + 1)
            pool.dma_start(xt[0][:, :, :], xview[0, 0]).then_inc(loaded_x[0], 16)

        @block.vector
        def _(dve):
            dve.sem_inc(xn_done, 2)
            dve.sem_inc(x_out, 2 * DT)
            dve.sem_inc(stored_x[0], 16)
            dve.sem_inc(stored_x[1], 16)

            def normalize(i, n, nth):
                x = xt[i]
                dve.wait_ge(loaded_x[i], nth * 16 + 16)
                for j in range(JT):
                    last = dve.bn_stats(stats[:, j, :], x[:, j, :])
                last.then_inc(stats_done, 1)
                dve.wait_ge(stats_done, n + 1)
                hold(dve, k)
                for j in range(JT):
                    last = dve.bn_aggr(mv[:, j, :], stats[:, j, :])
                last.then_inc(mv_done, 1)
                dve.wait_ge(rstd_done, n + 1)
                dve.wait_ge(turned, n * KD + KD)
                for j in range(JT):
                    last = dve.tensor_scalar(xn[:, j, :], x[:, j, :], mv[:, j, 0:1], rstd[:, j:j + 1],
                                             ALU.subtract, ALU.mult)
                last.then_inc(xn_done, 1)

            def copy_turned(i, n):
                dve.wait_ge(x_mm, n * DT)
                dve.wait_ge(z_mm, n * DT)
                dve.wait_ge(turned, n * KD + KD + 2)
                dve.tensor_copy(hT[i][:, 1, :], turn[1][:, :]).then_inc(h_dve, 1)

            normalize(0, 0, 0)
            copy_turned(0, 0)
            with dve.Fori(0, B) as b:
                for c in range(NC):
                    t, i = b * NC + c, c % 2
                    normalize(1 - i, t + 1, b * (NC // 2) + (c + 1) // 2)
                    dve.wait_ge(stored_x[i], b * (NC // 2) * 16 + c // 2 * 16 + 16)
                    for m in range(DT):
                        if m == 2:
                            copy_turned(1 - i, t + 1)
                        dve.wait_ge(x_mm, t * DT + m + 1 + 2 * DT)
                        dve.tensor_copy(out_x[i][:, m, :], mmx[m % 2][:, :]).then_inc(x_out, 1)

        @block.scalar
        def _(act):
            act.sem_inc(z_out, 2 * DT)
            act.sem_inc(stored_z[0], 16)
            act.sem_inc(stored_z[1], 16)

            def serve_ln(n):
                act.preload_act_table_set(EXP_AND_LN)
                act.wait_ge(mv_done, n + 1)
                act.activation(rstd[:, :], mv[:, :, 1], ACT.Ln, bias=k["eps"][:, :]).then_inc(log_done, 1)
                act.wait_ge(log_done, n + 1)
                act.activation(rstd[:, :], rstd[:, :], ACT.Exp, scale=-0.5).then_inc(rstd_done, 1)

            def copy_turned(i, n):
                act.wait_ge(x_mm, n * DT)
                act.wait_ge(z_mm, n * DT)
                act.wait_ge(turned, n * KD + 1 + 2)
                act.activation(hT[i][:, 0, :], turn[0][:, :], ACT.Copy).then_inc(h_act, 1)

            serve_ln(0)
            copy_turned(0, 0)
            with act.Fori(0, B) as b:
                for c in range(NC):
                    t, i = b * NC + c, c % 2
                    serve_ln(t + 1)
                    act.wait_ge(stored_z[i], b * (NC // 2) * 16 + c // 2 * 16 + 16)
                    for m in range(DT):
                        if m == 2:
                            copy_turned(1 - i, t + 1)
                        act.wait_ge(z_mm, t * DT + m + 1 + 2 * DT)
                        act.activation(out_z[i][:, m, :], mmz[m % 2][:, :], ACT.Silu).then_inc(z_out, 1)

        @block.tensor
        def _(pe):
            pe.sem_inc(turned, 2)
            pe.sem_inc(x_mm, 2 * DT)
            pe.sem_inc(z_mm, 2 * DT)
            pe.wait_ge(loaded_w, 16)

            def turn_rows(n):
                pe.wait_ge(xn_done, n + 3)
                pe.wait_ge(h_act, n)
                pe.wait_ge(h_dve, n)
                for q in range(KD):
                    for j in range(JT):
                        last = pe.transpose(turn[q][:, j * P:(j + 1) * P], xn[:, j, q * P:(q + 1) * P],
                                            k["ident"][:, :])
                    last.then_inc(turned, 1)

            turn_rows(0)
            with pe.Fori(0, B) as b:
                for c in range(NC):
                    t, h = b * NC + c, hT[c % 2]
                    pe.wait_ge(h_act, t + 1)
                    pe.wait_ge(h_dve, t + 1)
                    for m in range(DT):
                        if m == 2:
                            turn_rows(t + 1)
                        pe.wait_ge(x_out, t * DT + m + 1 + 2 * DT - 2)
                        for q in range(KD):
                            last = pe.matmul(mmx[m % 2][:, :], w[:, q, m * P:(m + 1) * P], h[:, q, :],
                                             start=q == 0, stop=q == KD - 1)
                        last.then_inc(x_mm, 1)
                        pe.wait_ge(z_out, t * DT + m + 1 + 2 * DT - 2)
                        for q in range(KD):
                            last = pe.matmul(mmz[m % 2][:, :], h[:, q, m * P:(m + 1) * P], w[:, q, DI:],
                                             start=q == 0, stop=q == KD - 1)
                        last.then_inc(z_mm, 1)



def scan_channels(nc, k, xin, y, convw, convb, xpw_dt, xpw_bc, dtw, dtb, alog, dskip):
    with Stage(nc, "scan") as s:
        xw = [s.sb(f"xw{i}", [P, DT, C + HALO]) for i in range(2)]
        diag = s.sb("diag", [P, 2, DT, TAPS, P])
        ddiag = s.sb("ddiag", [P, 2, DT, P])
        cw = s.sb("cw", [P, 2, DT, TAPS])
        cb = s.sb("cb", [P, 2, DT])
        db = s.sb("db", [P, 2, DT])
        dk = s.sb("dk", [P, 2, DT])
        an = s.sb("an", [P, 2, DT, NS])
        wdt = s.sb("wdt", [P, 2, DT, RANK])
        wbc = s.sb("wbc", [P, 2, DT, 96])
        wrk = s.sb("wrk", [RANK, 2, DI])
        pick = s.sb("pick", [96, 2, NS, P], BF16)
        xc = [s.sb(f"xc{i}", [P, DT, C]) for i in range(2)]
        dt = [s.sb(f"dt{i}", [P, DT, C]) for i in range(2)]
        dtx = [s.sb(f"dtx{i}", [P, DT, C]) for i in range(2)]
        ee = s.sb("ee", [P, DT, C])
        uu = s.sb("uu", [P, DT, C])
        rk = s.sb("rk", [RANK, C])
        bc = s.sb("bc", [96, C])
        bc_r = s.sb("bc_r", [96, C])
        bc_m = s.sb("bc_m", [96, C], BF16)
        split = [s.sb(f"split{i}", [96, C], BF16) for i in range(2)]
        dA = [s.sb(f"dA{i}", [P, DT, C]) for i in range(2)]
        dBx = [s.sb(f"dBx{i}", [P, DT, C]) for i in range(2)]
        hh = [s.sb(f"hh{i}", [P, DT, C]) for i in range(2)]
        hC = [s.sb(f"hC{i}", [P, DT, C]) for i in range(2)]
        cs = [s.sb(f"cs{i}", [P, C]) for i in range(2)]
        ysb = s.sb("ysb", [P, JT, DI])
        state = s.sb("state", [P, 2, NS, DT])
        acc = s.ps("acc", [P, JT, DI])
        bps = s.ps("bps", [P, C])
        cps = s.ps("cps", [P, C])
        fr = [s.ps(f"fr{i}", [P, C]) for i in range(2)]
        loaded_x = s.sems("loaded_x0", "loaded_x1")
        (loaded_w, diags, a_raw, a_ready, conv_mm, conv_out, bc_mm, rk_mm, bc_out, rk_out, bc_h, bc_r1,
         bc_m1, bc_ok, dt_mm, dt_relu, e_ok, u_ok, v_ok, d_ok, ln_ok, dt_ok, front_ok,
         b_mm, c_mm, c_copied, da_ok, dbx_ok, h_ok, hc_ok, acc_ok, y_out, y_stored,
         zeroed, saved, silu_ok, skip_ok, picks) = s.sems(
            "loaded_w", "diags", "a_raw", "a_ready", "conv_mm", "conv_out", "bc_mm", "rk_mm", "bc_out",
            "rk_out", "bc_h", "bc_r1", "bc_m1", "bc_ok", "dt_mm", "dt_relu", "e_ok", "u_ok", "v_ok", "d_ok",
            "ln_ok", "dt_ok", "front_ok", "b_mm", "c_mm", "c_copied", "da_ok", "dbx_ok", "h_ok",
            "hc_ok", "acc_ok", "y_out", "y_stored", "zeroed", "saved", "silu_ok", "skip_ok", "picks")
        NW = 8
        xinv = ch_view(xin)
        block = s.block()
        UNITS = B * NC * 2

        def all_units(eng, body):
            with eng.Fori(0, B) as b:
                with eng.Fori(0, NC) as c:
                    for d in range(2):
                        body(b, c, d, (b * NC + c) * 2 + d)

        @block.sync
        def _(sp):
            for dst, src in ((cw[:, :, :, :], convw), (cb[:, :, :], convb), (db[:, :, :], dtb), (dk[:, :, :], dskip),
                             (an[:, :, :, :], alog), (wdt[:, :, :, :], xpw_dt), (wbc[:, :, :, :], xpw_bc),
                             (wrk[:, :, :], dtw)):
                sp.dma_start(dst, src).then_inc(loaded_w, 16)

            def load(b, c, d, f):
                sp.wait_ge(conv_out, f * DT)
                hold(sp, k)
                at = c * C if d == 0 else (NC - 1 - c) * C + HALO
                sp.dma_start(xw[d][:, :, :], xinv[b][:, :, bass.ds(at, C + HALO)]).then_inc(loaded_x[d], 16)

            all_units(sp, load)
            for d in range(2):
                sp.wait_ge(conv_out, (UNITS + d) * DT)
                sp.dma_start(xw[d][:, :, :], xinv[0][:, :, 0:C + HALO]).then_inc(loaded_x[d], 16)

        @block.gpsimd
        def _(pool):
            pool.memset(pick[:, :, :, :], 0.0).then_inc(picks, 1)
            for part in range(3):
                pool.wait_ge(picks, part + 1)
                rows = pick[:, :, :, :].rearrange("r w n p -> r (w n) p")
                pool.affine_select(out=rows, in_=rows, compare_op=ALU.not_equal, fill=1.0, base=-32 * part,
                                   pattern=[[-1, 2 * NS], [0, P]], channel_multiplier=1).then_inc(picks, 1)
            pool.sem_inc(hc_ok, 2)
            pool.sem_inc(saved, 2)

            def front_relu_and_e(d, f):
                pool.wait_ge(e_ok, f + 1)
                pool.wait_ge(dt_relu, (f + 1) * DT)
                pool.tensor_tensor(dt[d][:, :, :], dt[d][:, :, :], ee[:, :, :], ALU.add).then_inc(v_ok, 1)

            front_relu_and_e(0, 0)
            with pool.Fori(0, B) as b:
                pool.wait_ge(saved, b * (2 * NC * NS) + 2)
                hold(pool, k)
                pool.memset(state[:, :, :, :], 0.0).then_inc(zeroed, 1)
                pool.wait_ge(zeroed, b + 1)
                hold(pool, k)
                with pool.Fori(0, NC) as c:
                    for d in range(2):
                        s0 = ((b * NC + c) * 2 + d) * NS
                        for n in range(NS):
                            pool.wait_ge(h_ok, s0 + n + 3)
                            pool.wait_ge(c_copied, s0 + n + 1)
                            pool.wait_ge(acc_ok, s0 + n + 1)
                            hold(pool, k)
                            last = C - 1 if d == 0 else 0
                            pool.tensor_copy(state[:, d, n, :], hh[n % 2][:, :, last]).then_inc(saved, 1)
                            pool.tensor_tensor(hC[n % 2][:, :, :], hh[n % 2][:, :, :],
                                               cs[n % 2][:, :].unsqueeze(1).broadcast_to([P, DT, C]),
                                               ALU.mult).then_inc(hc_ok, 1)
                            if n == 12:
                                front_relu_and_e(1 - d, (b * NC + c) * 2 + d + 1)

        @block.scalar
        def _(act):
            def front_conv(d, f, m):
                if m == 0 and not (isinstance(f, int) and f == 0):
                    act.wait_ge(skip_ok, f - 1)
                    act.wait_ge(front_ok, f - 1)
                act.wait_ge(conv_mm, f * DT + m + 1)
                act.activation(xc[d][:, m, :], fr[m % 2][:, :], ACT.Identity, bias=cb[:, d, m:m + 1]
                               ).then_inc(conv_out, 1)

            def front_silu(d, f):
                act.wait_ge(conv_out, (f + 2) * DT)
                act.activation(xc[d][:, :, :], xc[d][:, :, :], ACT.Silu).then_inc(silu_ok, 1)
                act.preload_act_table_set(EXP_AND_LN)

            def front_bc(d, f):
                act.wait_ge(bc_r1, f)
                act.wait_ge(bc_mm, f + 1)
                act.activation(bc[:, :], fr[0][0:96, :], ACT.Copy).then_inc(bc_out, 1)

            def front_rk(d, f):
                act.wait_ge(rk_mm, f + 1)
                act.activation(rk[:, :], fr[1][0:RANK, :], ACT.Copy).then_inc(rk_out, 1)

            def front_dt(d, f, m):
                if m == 0:
                    act.wait_ge(dt_ok, f)
                act.wait_ge(dt_mm, f * DT + m + 1)
                act.activation(ee[:, m, :], fr[m % 2][:, :], ACT.Abs, bias=db[:, d, m:m + 1])
                act.activation(dt[d][:, m, :], fr[m % 2][:, :], ACT.Relu, bias=db[:, d, m:m + 1]
                               ).then_inc(dt_relu, 1)

            def front_exp(f):
                act.wait_ge(dt_relu, (f + 1) * DT)
                act.activation(ee[:, :, :], ee[:, :, :], ACT.Exp, scale=-1.0).then_inc(e_ok, 1)

            def front_one_plus(f):
                act.wait_ge(e_ok, f + 1)
                act.wait_ge(d_ok, f)
                act.activation(uu[:, :, :], ee[:, :, :], ACT.Identity, bias=k["one"][:, :]).then_inc(u_ok, 1)

            def front_log(d, f):
                act.wait_ge(u_ok, f + 1)
                act.activation(dtx[d][:, :, :], uu[:, :, :], ACT.Ln).then_inc(ln_ok, 1)

            def front_all(d, f):
                for m in range(DT):
                    front_conv(d, f, m)
                front_silu(d, f)
                front_bc(d, f)
                front_rk(d, f)
                for m in range(DT):
                    front_dt(d, f, m)
                front_exp(f)
                front_one_plus(f)
                front_log(d, f)

            act.sem_inc(conv_out, DT)
            act.wait_ge(a_raw, 1)
            act.activation(an[:, :, :, :], an[:, :, :, :], ACT.Exp).then_inc(a_raw, 1)
            front_all(0, 0)
            act.wait_ge(a_ready, 1)

            def evacuate(f):
                act.wait_ge(acc_ok, f * NS + 2)
                act.wait_ge(y_stored, f * 16 + 16)
                act.activation(ysb[:, :, :], acc[:, :, :], ACT.Copy).then_inc(y_out, 1)

            def store(f):
                act.wait_ge(y_out, f + 1)
                act.dma_start(y[f], ysb[:, :, :]).then_inc(y_stored, 16)

            def decay(d, s0, n):
                act.wait_ge(h_ok, s0 + n + 1)
                for m in range(DT):
                    last = act.activation(dA[n % 2][:, m, :], dt[d][:, m, :], ACT.Exp, scale=an[:, d, m, n:n + 1])
                last.then_inc(da_ok, 1)

            def c_rows(s0, n):
                act.wait_ge(c_mm, s0 + n + 1)
                act.wait_ge(hc_ok, s0 + n + 1)
                act.activation(cs[n % 2][:, :], cps[:, :], ACT.Copy).then_inc(c_copied, 1)

            def unit(b, c, d, f):
                s0, o, g = f * NS, 1 - d, f + 1
                for n in range(NS):
                    if n + 1 < NS:
                        decay(d, s0, n + 1)
                    else:
                        act.wait_ge(dt_ok, g + 1)
                        decay(o, s0 + NS, 0)
                    if n == 0:
                        evacuate(f)
                    if n == 14:
                        front_log(o, g)
                    if n + 1 < NS:
                        c_rows(s0, n + 1)
                    else:
                        c_rows(s0 + NS, 0)
                    if n == 0:
                        front_conv(o, g, 0)
                        front_conv(o, g, 1)
                    if n == 2:
                        store(f)
                    if n == 3:
                        front_conv(o, g, 2)
                    if n == 4:
                        front_conv(o, g, 3)
                    if n == 5:
                        front_silu(o, g)
                    if n == 7:
                        front_bc(o, g)
                    if n == 8:
                        front_rk(o, g)
                    if n in (10, 11):
                        for m in range(2 * n - 20, 2 * n - 18):
                            front_dt(o, g, m)
                    if n == 12:
                        front_exp(g)
                    if n == 13:
                        front_one_plus(g)

            act.wait_ge(front_ok, 1)
            act.preload_act_table_set(EXP_AND_LN)
            decay(0, 0, 0)
            c_rows(0, 0)
            all_units(act, unit)
            evacuate(UNITS)
            store(UNITS)
            act.wait_ge(y_stored, 16 * (UNITS + 2))

        @block.vector
        def _(dve):
            dve.wait_ge(loaded_w, 16 * NW)
            dve.sem_inc(y_stored, 16)
            dve.sem_inc(h_ok, 2)
            dve.tensor_scalar(an[:, :, :, :], an[:, :, :, :], 80.0, None, ALU.min).then_inc(a_raw, 1)
            for d in range(2):
                for m in range(DT):
                    for j in range(TAPS):
                        dve.tensor_scalar(diag[:, d, m, j, :], k["ident"][:, :], cw[:, d, m, j:j + 1], None, ALU.mult)
                    dve.tensor_scalar(ddiag[:, d, m, :], k["ident"][:, :], dk[:, d, m:m + 1], None, ALU.mult)
            dve.memset(acc[:, :, :], 0.0).then_inc(diags, 1)
            dve.wait_ge(a_raw, 2)
            dve.tensor_scalar(an[:, :, :, :], an[:, :, :, :], -1.0, None, ALU.mult).then_inc(a_ready, 1)

            def front_split(d, f):
                dve.wait_ge(bc_out, f + 1)
                sp = split[d]
                dve.tensor_copy(sp[:, :], bc[:, :]).then_inc(bc_h, 1)
                dve.wait_ge(bc_h, f + 1)
                dve.tensor_tensor(bc_r[:, :], bc[:, :], sp[:, :], ALU.subtract).then_inc(bc_r1, 1)
                dve.wait_ge(bc_r1, f + 1)
                dve.tensor_copy(sp[32:64, :], bc_r[32:64, :])
                dve.tensor_copy(bc_m[64:96, :], bc_r[64:96, :]).then_inc(bc_m1, 1)
                dve.wait_ge(bc_m1, f + 1)
                dve.tensor_tensor(sp[64:96, :], bc_r[64:96, :], bc_m[64:96, :], ALU.subtract).then_inc(bc_ok, 1)

            def front_softplus(d, f):
                dve.wait_ge(u_ok, f + 1)
                dve.wait_ge(v_ok, f + 1)
                dve.scalar_tensor_tensor(out=ee[:, :, :], in0=uu[:, :, :], scalar=-1.0, in1=dt[d][:, :, :],
                                         op0=ALU.add, op1=ALU.subtract).then_inc(d_ok, 1)
                dve.wait_ge(ln_ok, f + 1)
                dve.wait_ge(d_ok, f + 1)
                dve.scalar_tensor_tensor(out=dt[d][:, :, :], in0=dtx[d][:, :, :], scalar=0.0, in1=ee[:, :, :],
                                         op0=ALU.max, op1=ALU.subtract).then_inc(dt_ok, 1)
                dve.wait_ge(dt_ok, f + 1)
                dve.tensor_tensor(dtx[d][:, :, :], dt[d][:, :, :], xc[d][:, :, :], ALU.mult).then_inc(front_ok, 1)

            def front_all(d, f):
                front_split(d, f)
                front_softplus(d, f)

            front_all(0, 0)
            dve.wait_ge(front_ok, 1)

            def inject(d, s0, n):
                dve.wait_ge(h_ok, s0 + n + 1)
                dve.wait_ge(b_mm, s0 + n + 1)
                dve.tensor_tensor(dBx[n % 2][:, :, :], dtx[d][:, :, :],
                                  bps[:, :].unsqueeze(1).broadcast_to([P, DT, C]), ALU.mult).then_inc(dbx_ok, 1)

            def scan(d, s0, n):
                dve.wait_ge(dbx_ok, s0 + n + 1)
                dve.wait_ge(da_ok, s0 + n + 1)
                dve.wait_ge(saved, s0 + n + 1)
                dve.wait_ge(hc_ok, s0 + n + 1)
                r = slice(None) if d == 0 else slice(None, None, -1)
                for m in range(DT):
                    last = dve.tensor_tensor_scan(hh[n % 2][:, m, r], dA[n % 2][:, m, r], dBx[n % 2][:, m, r],
                                                  state[:, d, n, m:m + 1], ALU.mult, ALU.add)
                last.then_inc(h_ok, 1)

            def unit(b, c, d, f):
                s0, o, g = f * NS, 1 - d, f + 1
                dve.wait_ge(zeroed, b + 1)
                for n in range(NS):
                    if n + 1 < NS:
                        inject(d, s0, n + 1)
                    else:
                        dve.wait_ge(front_ok, g + 1)
                        inject(o, s0 + NS, 0)
                    scan(d, s0, n)
                    if n == 8:
                        front_split(o, g)
                    if n == 14:
                        front_softplus(o, g)

            inject(0, 0, 0)
            all_units(dve, unit)
            dve.wait_ge(dbx_ok, UNITS * NS + 1)
            dve.sem_inc(dbx_ok, 1)

        @block.tensor
        def _(pe):
            pe.wait_ge(loaded_w, 16 * NW)
            pe.sem_inc(acc_ok, 2)
            pe.wait_ge(diags, 1)

            def front_conv(d, f, nth, taps):
                for m, j in taps:
                    if j == 0:
                        if m == 0:
                            pe.wait_ge(loaded_x[d], nth * 16 + 16)
                        if m >= 2:
                            pe.wait_ge(conv_out, (f + 1) * DT + m - 1)
                        elif not (isinstance(f, int) and f == 0):
                            pe.wait_ge(dt_relu, (f - 1) * DT + m + 3)
                    o = j if d == 0 else HALO - j
                    last = pe.matmul(fr[m % 2][:, :], diag[:, d, m, j, :], xw[d][:, m, o:o + C],
                                     start=j == 0, stop=j == TAPS - 1)
                    if j == TAPS - 1:
                        last.then_inc(conv_mm, 1)

            def front_proj(d, f, steps):
                for which, m in steps:
                    if m == 0 and which == 0:
                        pe.wait_ge(silu_ok, f + 1)
                    rows, w = ((96, wbc), (RANK, wdt))[which]
                    last = pe.matmul(fr[which][0:rows, :], w[:, d, m, :], xc[d][:, m, :], start=m == 0,
                                     stop=m == DT - 1)
                    if m == DT - 1:
                        last.then_inc((bc_mm, rk_mm)[which], 1)

            def front_dt(d, f, m):
                if m == 0:
                    pe.wait_ge(bc_out, f + 1)
                    pe.wait_ge(rk_out, f + 1)
                if m >= 2:
                    pe.wait_ge(dt_relu, f * DT + m - 1)
                pe.matmul(fr[m % 2][:, :], wrk[:, d, m * P:(m + 1) * P], rk[:, :], start=True, stop=True
                          ).then_inc(dt_mm, 1)

            all_taps = [(m, j) for m in range(DT) for j in range(TAPS)]
            all_steps = [(which, m) for which in range(2) for m in range(DT)]
            front_conv(0, 0, 0, all_taps)
            front_proj(0, 0, all_steps)
            for m in range(DT):
                front_dt(0, 0, m)
            front_conv(1, 1, 0, all_taps[0:8])

            def b_row(d, s0, n):
                pe.wait_ge(dbx_ok, s0 + n)
                pe.matmul(bps[:, :], pick[:, 0, n, :], split[d][:, :], start=True, stop=True).then_inc(b_mm, 1)

            def c_row(d, s0, n):
                pe.wait_ge(c_copied, s0 + n)
                pe.matmul(cps[:, :], pick[:, 1, n, :], split[d][:, :], start=True, stop=True).then_inc(c_mm, 1)

            def add(s0, n):
                pe.wait_ge(hc_ok, s0 + n + 3)
                for j in range(JT):
                    for m in range(DT):
                        last = pe.matmul(acc[:, j, m * P:(m + 1) * P], hC[n % 2][:, m, j * P:(j + 1) * P],
                                         k["ident"][:, :], start=n == 0 and m == 0, stop=False, is_transpose=True,
                                         skip_group_check=True)
                last.then_inc(acc_ok, 1)

            def skip(d, j):
                for m in range(DT):
                    last = pe.matmul(acc[:, j, m * P:(m + 1) * P], xc[d][:, m, j * P:(j + 1) * P],
                                     ddiag[:, d, m, :], start=False, stop=False, skip_group_check=True)
                if j == JT - 1:
                    last.then_inc(skip_ok, 1)

            late_taps = {1: all_taps[8:11], 2: all_taps[11:14], 3: all_taps[14:16]}
            steps = {6: all_steps[0:4], 7: all_steps[4:8]}
            early_taps = {13: all_taps[0:3], 14: all_taps[3:6], 15: all_taps[6:8]}
            skips = {4: 0, 8: 1, 11: 2, 12: 3}

            def unit(b, c, d, f):
                s0, o, g = f * NS, 1 - d, f + 1
                for n in range(NS):
                    if n + 2 < NS:
                        c_row(d, s0, n + 2)
                    else:
                        c_row(o, s0 + NS, n + 2 - NS)
                    front_conv(o, g, 0, late_taps.get(n, []))
                    front_proj(o, g, steps.get(n, []))
                    if n in (9, 10):
                        for m in range(2 * n - 18, 2 * n - 16):
                            front_dt(o, g, m)
                    front_conv(d, f + 2, b * NC + c + 1, early_taps.get(n, []))
                    if n + 3 < NS:
                        b_row(d, s0, n + 3)
                    else:
                        if n + 3 == NS:
                            pe.wait_ge(bc_ok, f + 2)
                        b_row(o, s0 + NS, n + 3 - NS)
                    if n == 0:
                        pe.wait_ge(y_out, f + 1)
                    add(s0, n)
                    if n in skips:
                        skip(d, skips[n])

            pe.wait_ge(bc_ok, 1)
            pe.wait_ge(picks, 4)
            for n in range(2):
                b_row(0, 0, n)
                c_row(0, 0, n)
            b_row(0, 0, 2)
            all_units(pe, unit)


def scan_layouts(i):
    import numpy as np

    def both(name, lay):
        return np.ascontiguousarray(np.stack([lay(np.asarray(i[f"{d}_{name}"])) for d in ("fwd", "bwd")], 1))

    def vec(a):
        return a.reshape(DT, P).T

    def rows(a):
        return a.T.reshape(DT, P, -1).transpose(1, 0, 2)

    return {
        "convw": both("conv_w", lambda a: rows(a[:, 0, :].T)),
        "convb": both("conv_b", vec),
        "xpw_dt": both("x_proj_w", lambda a: rows(a[:RANK])),
        "xpw_bc": both("x_proj_w", lambda a: rows(np.concatenate([a[RANK:]] * 3))),
        "dtw": both("dt_w", lambda a: a.T),
        "dtb": both("dt_b", vec),
        "alog": both("A_log", lambda a: rows(a.T)),
        "dskip": both("D", vec),
    }



def mix_and_qkv(nc, k, y, sz, u, out_wT, g1, b1, wqkv, rope, x1, xf, qk, va):
    with Stage(nc, "mix") as s:
        yf = [s.sb(f"yf{i}", [P, JT, DI]) for i in range(2)]
        yb = [s.sb(f"yb{i}", [P, JT, DI]) for i in range(2)]
        z = [s.sb(f"z{i}", [P, JT, DI]) for i in range(2)]
        ut = [s.sb(f"ut{i}", [P, JT, D]) for i in range(2)]
        tab = s.sb("tab", [P, 2, NC, JT, 2, HD // 2])
        gated = s.sb("gated", [P, JT, DI])
        gT = s.sb("gT", [P, DT, C])
        wo = s.sb("wo", [P, DT, D])
        wq = s.sb("wq", [P, KD, 3 * D])
        gb = s.sb("gb", [P, 2, D])
        stats = s.sb("stats", [P, 3, JT, 6])
        mv = s.sb("mv", [P, 3, JT, 2])
        rstd = s.sb("rstd", [P, 3, JT])
        x1t = s.sb("x1t", [P, JT, D])
        xft = s.sb("xft", [P, JT, D])
        ht = s.sb("ht", [P, JT, D])
        hT = s.sb("hT", [P, KD, C])
        rc = [s.sb(f"rc{i}", [P, 2, 2, H, HD // 2]) for i in range(2)]
        rs = [s.sb(f"rs{i}", [P, 2, 2, H, HD // 2]) for i in range(2)]
        rot = [s.sb(f"rot{i}", [P, 2, H, HD]) for i in range(2)]
        rest = [s.sb(f"rest{i}", [P, 2, H, HD]) for i in range(2)]
        parts = s.sb("parts", [P, JT, 2, H, 6, HD], BF16)
        vt = [s.sb(f"vt{i}", [P, JT, H, HD + 1]) for i in range(2)]
        heads = [s.sb(f"heads{i}", [STACK, 4, 2, C], BF16) for i in range(H // 4)]
        turn = [s.ps(f"turn{i}", [P, C]) for i in range(2)]
        po = s.ps("po", [P, JT, D])
        pqk = s.ps("pqk", [P, 2, 2, H, HD // 2])
        pv = s.ps("pv", [P, D])
        ph = [s.ps(f"ph{i}", [STACK, 2, C], BF16) for i in range(2)]
        loaded = s.sems("loaded0", "loaded1")
        stored_v = s.pool_dma_sems("stored_v0", "stored_v1")
        stored_h = s.sems(*[f"stored_h{i}" for i in range(H // 4)])
        (loaded_w, summed, gated_ok, g_turned, g_out, o_mm, st_ok, mv_ok, log_ok, rstd_ok, n_ok, x1_ok, h_ok,
         h_turned, h_out, qk_mm, v_mm, rc_ok, rot_ok, hi_ok, rest_ok, mid_ok, lo_ok, spread, v_out, hd_turned,
         hd_out, ones_ok, x1_read) = s.sems(
            "loaded_w", "summed", "gated_ok", "g_turned", "g_out", "o_mm", "st_ok", "mv_ok", "log_ok", "rstd_ok",
            "n_ok", "x1_ok", "h_ok", "h_turned", "h_out", "qk_mm", "v_mm", "rc_ok", "rot_ok", "hi_ok", "rest_ok",
            "mid_ok", "lo_ok", "spread", "v_out", "hd_turned", "hd_out", "ones_ok", "x1_read")
        stored_x1, stored_xf = s.pool_dma_sems("stored_x1", "stored_xf")
        NW = 6
        HB = NC // 2
        szv, uv, x1v, xfv = tok_view(sz), tok_view(u), tok_view(x1), tok_view(xf)
        vav = tok_view(va)
        block = s.block()

        LAST = B * NC - 1

        def chunks(eng, body):
            with eng.Fori(0, B) as b:
                for c in range(NC):
                    body(b, c, b * NC + c)

        @block.sync
        def _(sp):
            for dst, src in ((wo[:, :, :], out_wT.rearrange("(k p) m -> p k m", p=P)),
                             (wq[:, :, :], wqkv.rearrange("(k p) m -> p k m", p=P)),
                             (gb[:, 0, :], g1.broadcast_to([P, D])), (gb[:, 1, :], b1.broadcast_to([P, D])),
                             (tab[:, 0, :, :, :, :], rope[0]), (tab[:, 1, :, :, :, :], rope[1])):
                sp.dma_start(dst, src).then_inc(loaded_w, 16)

            def load(b, c, t):
                i = t % 2 if isinstance(t, int) else c % 2
                sp.wait_ge(x1_read, t + 1)
                sp.wait_ge(gated_ok, t + 1)
                sp.dma_start(yf[i][:, :, :], y[b * (2 * NC) + (2 * c + 1)]).then_inc(loaded[i], 16)
                sp.dma_start(yb[i][:, :, :], y[b * (2 * NC) + (2 * (NC - 1 - c) + 2)]).then_inc(loaded[i], 16)
                sp.dma_start(z[i][:, :, :], szv[b, c]).then_inc(loaded[i], 16)
                sp.dma_start(ut[i][:, :, :], uv[b, c]).then_inc(loaded[i], 16)

            chunks(sp, load)
            load(0, 0, LAST + 1)
            load(0, 0, LAST + 2)

        @block.gpsimd
        def _(pool):
            for i in range(2):
                pool.memset(vt[i][:, :, :, HD:], 1.0).then_inc(ones_ok, 1)
            pool.sem_inc(gated_ok, 2)
            pool.sem_inc(rest_ok, 1)
            pool.sem_inc(lo_ok, 1)

            def gate(i, n):
                pool.wait_ge(summed, n + 1)
                pool.wait_ge(g_turned, n * DT)
                pool.tensor_tensor(gated[:, :, :], yf[i][:, :, :], z[i][:, :, :], ALU.mult).then_inc(gated_ok, 1)

            def low(j, q):
                e = rest[j % 2]
                pool.wait_ge(mid_ok, q + 1)
                pool.tensor_tensor(parts[:, j, 0, :, 2, :], e[:, 0, :, :], parts[:, j, 0, :, 1, :], ALU.subtract)
                pool.tensor_tensor(parts[:, j, 1, :, 5, :], e[:, 1, :, :], parts[:, j, 1, :, 3, :], ALU.subtract
                                   ).then_inc(lo_ok, 1)

            gate(0, 0)
            gate(1, 1)

            def chunk(b, c, t):
                i = c % 2
                pool.wait_ge(x1_ok, t + 1)
                hold(pool, k)
                pool.dma_start(x1v[b, c], x1t[:, :, :]).then_inc(stored_x1, 16)
                pool.wait_ge(n_ok, t * 3 + 2)
                hold(pool, k)
                pool.dma_start(xfv[b, c], xft[:, :, :]).then_inc(stored_xf, 16)
                for j in range(JT):
                    q = t * JT + j
                    pool.wait_ge(hi_ok, q + 1)
                    pool.wait_ge(lo_ok, q)
                    pool.tensor_tensor(rest[j % 2][:, :, :, :], rot[j % 2][:, :, :, :], parts[:, j, :, :, 0, :],
                                       ALU.subtract).then_inc(rest_ok, 1)
                    if j:
                        low(j - 1, q - 1)
                low(JT - 1, t * JT + JT - 1)
                pool.wait_ge(v_out, t * JT + JT)
                hold(pool, k)
                pool.dma_start(vav[b, c].rearrange("p j (h e) -> p j h e", h=H), vt[i][:, :, :, :]
                               ).then_inc(stored_v[i], 16)
                gate(i, t + 2)

            chunks(pool, chunk)
            pool.wait_ge(stored_x1, 16 * B * NC)
            pool.wait_ge(stored_xf, 16 * B * NC)
            for i in range(2):
                pool.wait_ge(stored_v[i], 16 * B * HB)

        @block.vector
        def _(dve):
            dve.wait_ge(loaded_w, 16 * NW)
            dve.sem_inc(x1_read, 2)

            def measure(src, which, n):
                for j in range(JT):
                    last = dve.bn_stats(stats[:, which, j, :], src[:, j, :])
                last.then_inc(st_ok, 1)
                dve.wait_ge(st_ok, n + 1)
                hold(dve, k)
                for j in range(JT):
                    last = dve.bn_aggr(mv[:, which, j, :], stats[:, which, j, :])
                last.then_inc(mv_ok, 1)

            def normalize(dst, src, which, n):
                dve.wait_ge(rstd_ok, n + 1)
                for j in range(JT):
                    last = dve.tensor_scalar(dst[:, j, :], src[:, j, :], mv[:, which, j, 0:1],
                                             rstd[:, which, j:j + 1], ALU.subtract, ALU.mult)
                last.then_inc(n_ok, 1)
                dve.wait_ge(n_ok, n + 1)

            def add_up(i, n, nth):
                dve.wait_ge(loaded[i], nth * 64 + 64)
                dve.tensor_tensor(yf[i][:, :, :], yf[i][:, :, :], yb[i][:, :, :], ALU.add).then_inc(summed, 1)

            def begin_x1(n):
                dve.wait_ge(o_mm, n + 1)
                measure(po, 0, n * 3)

            def make_x1(i, n):
                dve.wait_ge(stored_x1, n * 16)
                normalize(x1t, po, 0, n * 3)
                dve.tensor_tensor(x1t[:, :, :], x1t[:, :, :], ut[i][:, :, :], ALU.add).then_inc(x1_ok, 1)
                dve.wait_ge(x1_ok, n + 1)
                dve.sem_inc(x1_read, 1)
                measure(x1t, 1, n * 3 + 1)

            def make_xf(n):
                dve.wait_ge(stored_xf, n * 16)
                normalize(xft, x1t, 1, n * 3 + 1)
                measure(xft, 2, n * 3 + 2)

            def make_h(n):
                dve.wait_ge(h_turned, n * KD)
                normalize(ht, xft, 2, n * 3 + 2)
                dve.tensor_tensor(ht[:, :, :], ht[:, :, :], gb[:, 0:1, :].broadcast_to([P, JT, D]), ALU.mult
                                  ).then_inc(h_ok, 1)
                dve.wait_ge(h_ok, n * 2 + 1)
                dve.tensor_tensor(ht[:, :, :], ht[:, :, :], gb[:, 1:2, :].broadcast_to([P, JT, D]), ALU.add
                                  ).then_inc(h_ok, 1)

            def middle(j, q):
                e = rest[j % 2]
                dve.wait_ge(rest_ok, q + 2)
                dve.tensor_copy(parts[:, j, 0, :, 1, :], e[:, 0, :, :])
                dve.tensor_copy(parts[:, j, 1, :, 3, :], e[:, 1, :, :]).then_inc(mid_ok, 1)

            add_up(0, 0, 0)
            add_up(1, 1, 0)
            begin_x1(0)
            make_x1(0, 0)
            make_xf(0)
            make_h(0)

            def chunk(b, c, t):
                i, nth = c % 2, b * HB + c // 2
                for j in range(JT):
                    q = t * JT + j
                    co, si, r = rc[j % 2], rs[j % 2], rot[j % 2]
                    dve.wait_ge(qk_mm, q + 1)
                    for dst, which in ((co, 0), (si, 1)):
                        last = dve.tensor_tensor(
                            dst[:, :, :, :, :].rearrange("p w f h e -> p w (f h) e"),
                            pqk[:, :, :, :, :].rearrange("p w f h e -> p w (f h) e"),
                            tab[:, which, c, j, :, :].unsqueeze(2).broadcast_to([P, 2, 2 * H, HD // 2]), ALU.mult)
                    last.then_inc(rc_ok, 1)
                    dve.wait_ge(rc_ok, q + 1)
                    dve.wait_ge(rest_ok, q)
                    dve.tensor_tensor(r[:, :, :, 0:HD // 2], co[:, :, 0, :, :], si[:, :, 1, :, :], ALU.subtract)
                    dve.tensor_tensor(r[:, :, :, HD // 2:], si[:, :, 0, :, :], co[:, :, 1, :, :], ALU.add
                                      ).then_inc(rot_ok, 1)
                    dve.wait_ge(rot_ok, q + 1)
                    dve.wait_ge(hd_turned, t * H)
                    dve.tensor_copy(parts[:, j, :, :, 0, :], r[:, :, :, :]).then_inc(hi_ok, 1)
                    if j:
                        middle(j - 1, q - 1)
                middle(JT - 1, t * JT + JT - 1)
                add_up(i, t + 2, nth + 1)
                begin_x1(t + 1)
                make_x1(1 - i, t + 1)
                make_xf(t + 1)
                make_h(t + 1)

            chunks(dve, chunk)

        @block.scalar
        def _(act):
            act.wait_ge(ones_ok, 2)
            act.sem_inc(hd_out, 1)
            RSTD_AT = (0, 5, 9)

            def store_heads(b, c, t, g):
                act.wait_ge(hd_out, t * H + 4 * g + 5)
                for w in range(2):
                    act.dma_start(qk[b, 4 * g:4 * g + 4, w, :, c * C:c * C + C].rearrange("h r l -> r h l"),
                                  heads[g][:, :, w, :]).then_inc(stored_h[g], 16)
            act.preload_act_table_set(EXP_AND_LN)

            def gated_copy(n, m):
                act.wait_ge(g_turned, n * DT + m + 1)
                act.wait_ge(o_mm, n)
                act.activation(gT[:, m, :], turn[m % 2][:, :], ACT.Copy).then_inc(g_out, 1)

            def rstd_of(which, n):
                act.wait_ge(mv_ok, n * 3 + which + 1)
                act.activation(rstd[:, which, :], mv[:, which, :, 1], ACT.Ln, bias=k["eps"][:, :]).then_inc(log_ok, 1)
                act.wait_ge(log_ok, n * 3 + which + 1)
                act.activation(rstd[:, which, :], rstd[:, which, :], ACT.Exp, scale=-0.5).then_inc(rstd_ok, 1)

            def h_copies(n):
                act.wait_ge(v_mm, n * JT)
                for m in range(KD):
                    act.wait_ge(h_turned, n * KD + m + 1)
                    act.activation(hT[:, m, :], turn[m % 2][:, :], ACT.Copy).then_inc(h_out, 1)

            def spread_parts(j, q):
                act.wait_ge(mid_ok, q + 1)
                pt = parts[:, j, :, :, :, :]
                act.activation(pt[:, 0, :, 3, :], pt[:, 0, :, 0, :], ACT.Copy)
                act.activation(pt[:, 0, :, 5, :], pt[:, 0, :, 0, :], ACT.Copy)
                act.activation(pt[:, 0, :, 4, :], pt[:, 0, :, 1, :], ACT.Copy)
                act.activation(pt[:, 1, :, 1, :], pt[:, 1, :, 0, :], ACT.Copy)
                act.activation(pt[:, 1, :, 2, :], pt[:, 1, :, 0, :], ACT.Copy)
                act.activation(pt[:, 1, :, 4, :], pt[:, 1, :, 3, :], ACT.Copy).then_inc(spread, 1)

            for m in range(DT):
                gated_copy(0, m)
            for which in range(3):
                rstd_of(which, 0)
            h_copies(0)

            def chunk(b, c, t):
                i, nth = c % 2, b * HB + c // 2
                for j in range(JT):
                    q = t * JT + j
                    act.wait_ge(v_mm, q + 1)
                    if j == 0:
                        act.wait_ge(stored_v[i], nth * 16)
                    act.activation(vt[i][:, j, :, 0:HD], pv[:, :].rearrange("p (h e) -> p h e", h=H), ACT.Copy
                                   ).then_inc(v_out, 1)
                    if j < 2:
                        gated_copy(t + 1, 2 * j)
                        gated_copy(t + 1, 2 * j + 1)
                    if j:
                        spread_parts(j - 1, q - 1)
                spread_parts(JT - 1, t * JT + JT - 1)
                for h in range(H):
                    g = h // 4
                    act.wait_ge(hd_turned, t * H + h + 1)
                    if h % 4 == 0:
                        act.wait_ge(stored_h[g], t * 32)
                    act.activation(heads[g][:, h % 4, :, :], ph[h % 2][:, :, :], ACT.Copy).then_inc(hd_out, 1)
                    if h % 4 == 0 and h:
                        store_heads(b, c, t, g - 1)
                    if h in RSTD_AT:
                        rstd_of(RSTD_AT.index(h), t + 1)
                store_heads(b, c, t, H // 4 - 1)
                h_copies(t + 1)

            chunks(act, chunk)
            for g in range(H // 4):
                act.wait_ge(stored_h[g], 32 * B * NC)

        @block.tensor
        def _(pe):
            pe.wait_ge(loaded_w, 16 * NW)

            def turn_gated(n, m):
                if m == 0:
                    pe.wait_ge(gated_ok, n + 3)
                    pe.wait_ge(h_out, n * KD)
                if m >= 2:
                    pe.wait_ge(g_out, n * DT + m - 1)
                for j in range(JT):
                    last = pe.transpose(turn[m % 2][:, j * P:(j + 1) * P], gated[:, j, m * P:(m + 1) * P],
                                        k["ident"][:, :])
                last.then_inc(g_turned, 1)

            def out_project(n):
                pe.wait_ge(g_out, n * DT + DT)
                pe.wait_ge(n_ok, n * 3)
                for j in range(JT):
                    for m in range(DT):
                        last = pe.matmul(po[:, j, :], gT[:, m, j * P:(j + 1) * P], wo[:, m, :], start=m == 0,
                                         stop=m == DT - 1)
                last.then_inc(o_mm, 1)

            def turn_h(n):
                pe.wait_ge(h_ok, n * 2 + 2)
                pe.wait_ge(g_out, n * DT + DT)
                for m in range(KD):
                    for j in range(JT):
                        last = pe.transpose(turn[m % 2][:, j * P:(j + 1) * P], ht[:, j, m * P:(m + 1) * P],
                                            k["ident"][:, :])
                    last.then_inc(h_turned, 1)

            for m in range(DT):
                turn_gated(0, m)
            out_project(0)
            turn_h(0)

            def chunk(b, c, t):
                pe.wait_ge(h_out, t * KD + KD)
                for j in range(JT):
                    q = t * JT + j
                    pe.wait_ge(rc_ok, q)
                    for m in range(KD):
                        last = pe.matmul(pqk[:, :, :, :, :].rearrange("p w f h e -> p (w f h e)"),
                                         hT[:, m, j * P:(j + 1) * P], wq[:, m, 0:2 * D], start=m == 0, stop=m == 1)
                    last.then_inc(qk_mm, 1)
                    pe.wait_ge(v_out, q)
                    for m in range(KD):
                        last = pe.matmul(pv[:, :], hT[:, m, j * P:(j + 1) * P], wq[:, m, 2 * D:], start=m == 0,
                                         stop=m == 1)
                    last.then_inc(v_mm, 1)
                    if j < 2:
                        turn_gated(t + 1, 2 * j)
                        turn_gated(t + 1, 2 * j + 1)
                    if j == JT - 1:
                        out_project(t + 1)
                pe.wait_ge(spread, t * JT + JT)
                pe.wait_ge(lo_ok, t * JT + JT + 1)
                for h in range(H):
                    pe.wait_ge(hd_out, t * H + h)
                    for w in range(2):
                        for j in range(JT):
                            last = pe.transpose(ph[h % 2][:, w, j * P:(j + 1) * P],
                                                parts[:, j, w, h, :, :].rearrange("p a e -> p (a e)"),
                                                k["identb"][:, :])
                    last.then_inc(hd_turned, 1)
                turn_h(t + 1)

            chunks(pe, chunk)


def rope_tables():
    import numpy as np
    inv = (1.0 / np.float32(10000.0) ** (np.arange(0, HD, 2, dtype=np.float32) / np.float32(HD))).astype(np.float32)
    ang = np.arange(L, dtype=np.float32)[:, None] * inv
    t = np.stack([np.cos(ang), np.sin(ang)]).astype(np.float32)
    t = np.stack([t * np.float32(HD ** -0.5), t], 2)
    return np.ascontiguousarray(t.reshape(2, NC, JT, P, 2, HD // 2).transpose(0, 3, 1, 2, 4, 5))


def qkv_layout(w):
    import numpy as np
    w = np.asarray(w).reshape(D, H, 3, 2, HD // 2)
    qk = w[:, :, 0:2].transpose(0, 2, 3, 1, 4).reshape(D, 2 * D)
    return np.ascontiguousarray(np.concatenate([qk, w[:, :, 2].reshape(D, D)], 1))



def attend(nc, k, qk, va, pick_heads, attnT):
    KT = L // P
    QUAD = C // P
    WIDE = 2 * C
    second = [(qc, quad, half) for qc in range(NC) for quad in range(qc + 1) for half in range(2)]
    N2 = len(second)
    ends = [max(i for i, x in enumerate(second) if x[0] == qc) for qc in range(NC)]
    ADD_AT = {ends[0] + 4: 0, ends[1] + 4: 1, ends[2] + 4: 2}
    units = [(t, c) for t in range(KT - 1, -1, -1) for c in range(t // JT + 1)]
    N1 = len(units)
    FROM, TO = 0, 18
    shares = [min(max(st - FROM, 0), TO - FROM) * N1 // (TO - FROM) for st in range(N2 + 1)]
    first = [units[shares[st]:shares[st + 1]] for st in range(N2)]
    before1 = [sum(len(f) for f in first[:st]) for st in range(N2)]
    assert sum(len(f) for f in first) == N1
    SPLIT_AT = max(st for st in range(N2) if first[st])
    TURN_AT = SPLIT_AT + 1
    PLACE_AT = TURN_AT + 1
    ROWS = STACK + 3
    SETS = 4
    with Stage(nc, "attend") as s:
        qt = [s.sb(f"qt{i}", [ROWS, L], BF16) for i in range(SETS)]
        kt_ = [s.sb(f"kt{i}", [ROWS, L], BF16) for i in range(SETS)]
        vall = s.sb("vall", [P, B * KT, H * (HD + 1)])
        vs = [s.sb(f"vs{i}", [P, KT, 32]) for i in range(2)]
        full = [s.sb(f"full{i}", [P, QUAD, C]) for i in range(2)]
        diag = [s.sb(f"diag{i}", [P, QUAD, C]) for i in range(2)]
        pick = s.sb("pick", [P, 2, 64])
        mx = s.sb("mx", [P, KT, JT])
        m = s.sb("m", [P, KT])
        mr = s.sb("mr", [P, KT])
        mparts = s.sb("mparts", [P, 3, KT], BF16)
        mrows = s.sb("mrows", [3 * KT, P], BF16)
        sums = [s.sb(f"sums{i}", [P, NC, C]) for i in range(2)]
        lden = s.sb("lden", [32, C])
        rden = s.sb("rden", [32, C])
        out = s.sb("out", [32, NC, C])
        s1 = [s.ps(f"s1_{i}", [P, C]) for i in range(2)]
        s2 = [s.ps(f"s2_{i}", [P, 2, C]) for i in range(2)]
        pv = s.ps("pv", [P, C])
        px = s.ps("px", [P, C])
        pm = s1[0][0:3 * KT, 0:P // 2].bitcast(BF16)
        loaded = s.sems(*[f"loaded{i}" for i in range(SETS)])
        (loaded_v, loaded_pick, mx_ok, ones_ok, filled, v_ok, s1_mm, s1_read, m_ok, hi_ok, mr_ok, mid_ok, lo_ok, m_turned,
         m_rows, m_in, s2_mm, s2_read, pv_ok, pv_out, added, lden_ok, rden_ok, out_ok) = s.sems(
            "loaded_v", "loaded_pick", "mx_ok", "ones_ok", "filled", "v_ok", "s1_mm", "s1_read", "m_ok", "hi_ok", "mr_ok",
            "mid_ok", "lo_ok", "m_turned", "m_rows", "m_in", "s2_mm", "s2_read", "pv_ok",
            "pv_out", "added", "lden_ok", "rden_ok", "out_ok")
        (stored,) = s.pool_dma_sems("stored")
        vav = va.rearrange("(t p) e -> p t e", p=P)
        NQ = N2 // 2
        quad_no = [i // 2 for i in range(N2)]

        def prob_buffer(st):
            qc, quad, _ = second[st]
            if quad == qc:
                return diag[qc % 2]
            return full[(qc * (qc - 1) // 2 + quad) % 2]

        def quads_back(st):
            own = prob_buffer(st)
            back = 1
            while prob_buffer((st - 2 * back) % N2) is not own:
                back += 1
            return back

        block = s.block()

        def heads(eng, body):
            with eng.Fori(0, B) as b:
                with eng.Fori(0, H // SETS) as turn:
                    for j in range(SETS):
                        hp = turn * (SETS // 2) + j // 2
                        body(b, hp, j % 2, b * H + turn * SETS + j, b * (H // 2) + hp, j, b * (H // SETS) + turn)

        @block.sync
        def _(sp):
            sp.dma_start(pick[:, :, :], pick_heads).then_inc(loaded_pick, 16)
            sp.dma_start(vall[:, :, :], vav).then_inc(loaded_v, 16)

            def load(src, j, n):
                sp.wait_ge(s2_mm, n * N2)
                sp.dma_start(qt[j][0:STACK, :], src[0]).then_inc(loaded[j], 16)
                sp.dma_start(kt_[j][0:STACK, :], src[1]).then_inc(loaded[j], 16)

            def head(b, hp, i, n, nth, j, turn):
                load((qk[b, hp * 2 + i, 0], qk[b, hp * 2 + i, 1]), j, n)

            heads(sp, head)
            for j in range(2):
                load((qk[0, j, 0], qk[0, j, 1]), j, B * H + j)

        @block.gpsimd
        def _(pool):
            for j in range(SETS):
                pool.memset(kt_[j][STACK:ROWS, :], 1.0).then_inc(ones_ok, 1)
                pool.wait_ge(ones_ok, j + 1)
            for i in range(2):
                pool.memset(diag[i][:, :, :], 0.0).then_inc(filled, 1)
                pool.memset(vs[i][:, :, :], 0.0).then_inc(filled, 1)

            def head(b, hp, i, n, nth, j, turn):
                if i == 1:
                    pool.wait_ge(out_ok, (nth + 1) * NC)
                    hold(pool, k)
                    pool.dma_start(attnT[b, bass.ds(hp * 32, 32), :].rearrange("r (c l) -> r c l", c=NC),
                                   out[:, :, :]).then_inc(stored, 16)

            heads(pool, head)
            pool.wait_ge(stored, 16 * B * H // 2)

        @block.vector
        def _(dve):
            dve.memset(mx[:, :, :], -3.0e38).then_inc(mx_ok, 1)
            dve.sem_inc(s1_read, 2)
            dve.wait_ge(loaded_v, 16)
            dve.wait_ge(filled, 4)
            dve.wait_ge(mx_ok, 1)

            def maxima(n1, st):
                for j, (t, c) in enumerate(first[st]):
                    v = before1[st] + j
                    w = min(C, (t + 1) * P - c * C)
                    dve.wait_ge(s1_mm, n1 * N1 + v + 1)
                    if v == 0:
                        dve.wait_ge(m_ok, n1)
                    dve.tensor_reduce(mx[:, t, c:c + 1], s1[v % 2][:, 0:w], AX_X, ALU.max).then_inc(s1_read, 1)

            def split_max(n1):
                dve.wait_ge(s1_read, (n1 + 1) * N1 + 2)
                dve.wait_ge(lo_ok, n1)
                dve.tensor_reduce(m[:, :], mx[:, :, :], AX_X, ALU.max).then_inc(m_ok, 1)
                dve.wait_ge(m_ok, n1 + 1)
                dve.wait_ge(m_turned, n1)
                dve.tensor_scalar(mparts[:, 0, :], m[:, :], -1.0, None, ALU.mult).then_inc(hi_ok, 1)
                dve.wait_ge(hi_ok, n1 + 1)
                dve.scalar_tensor_tensor(out=mr[:, :], in0=m[:, :], scalar=-1.0, in1=mparts[:, 0, :], op0=ALU.mult,
                                         op1=ALU.subtract).then_inc(mr_ok, 1)
                dve.wait_ge(mr_ok, n1 + 1)
                dve.tensor_copy(mparts[:, 1, :], mr[:, :]).then_inc(mid_ok, 1)
                dve.wait_ge(mid_ok, n1 + 1)
                dve.tensor_tensor(mparts[:, 2, :], mr[:, :], mparts[:, 1, :], ALU.subtract).then_inc(lo_ok, 1)

            def copy_rows(n1):
                dve.wait_ge(m_turned, n1 + 1)
                dve.wait_ge(m_in, n1 * 48)
                dve.tensor_copy(mrows[:, :], pm).then_inc(m_rows, 1)

            for n1 in range(2):
                for st in range(N2):
                    maxima(n1, st)
                split_max(n1)
                copy_rows(n1)

            def normalize(nth, qc):
                v = nth * NC + qc
                dve.wait_ge(rden_ok, v + 1)
                dve.wait_ge(stored, nth * 16)
                dve.tensor_tensor(out[:, qc, :], px[0:32, :], rden[:, :], ALU.mult).then_inc(out_ok, 1)

            def head(b, hp, i, n, nth, j, turn):
                dve.wait_ge(pv_ok, n * NQ)
                dve.tensor_copy(vs[i][:, :, 0:HD + 1],
                                vall[:, bass.ds(b * KT, KT), bass.ds((hp * 2 + i) * (HD + 1), HD + 1)]
                                ).then_inc(v_ok, 1)
                for st in range(N2):
                    maxima(n + 2, st)
                    if st == SPLIT_AT:
                        split_max(n + 2)
                    if i == 1 and st - 3 in ADD_AT:
                        normalize(nth, ADD_AT[st - 3])
                    if st == TURN_AT:
                        copy_rows(n + 2)
                if i == 1:
                    normalize(nth, NC - 1)

            heads(dve, head)

        @block.scalar
        def _(act):
            act.sem_inc(s2_read, 2)
            act.preload_act_table_set(EXP_AND_LN)
            act.wait_ge(filled, 4)

            def place_max(j, n):
                act.wait_ge(m_rows, n + 1)
                for part in range(3):
                    act.dma_start(qt[j][STACK + part:STACK + part + 1, :].rearrange("r (t q) -> r t q", q=P),
                                  mrows[part * KT:(part + 1) * KT, :]).then_inc(m_in, 16)

            for j in range(2):
                place_max(j, j)

            def evacuate(i, n, nth, qc):
                act.wait_ge(pv_ok, (n + 1) * NQ + (ends[qc] + 1) // 2)
                act.wait_ge(added, nth * NC)
                act.activation(sums[i][:, qc, :], pv[:, :], ACT.Copy).then_inc(pv_out, 1)

            def invert(nth, qc):
                v = nth * NC + qc
                act.wait_ge(added, v + 1)
                act.activation(lden[:, :], px[32:64, :], ACT.Ln).then_inc(lden_ok, 1)
                act.wait_ge(lden_ok, v + 1)
                act.wait_ge(out_ok, v)
                act.activation(rden[:, :], lden[:, :], ACT.Exp, scale=-1.0).then_inc(rden_ok, 1)

            def head(b, hp, i, n, nth, j, turn):
                for st, (qc, quad, half) in enumerate(second):
                    buf = prob_buffer(st)
                    if half == 0:
                        act.wait_ge(pv_ok, (n + 1) * NQ + quad_no[st] + 1 - quads_back(st))
                    act.wait_ge(s2_mm, (n + SETS - 1) * N2 + st + 1)
                    if quad < qc:
                        last = act.activation(buf[:, 2 * half:2 * half + 2, :], s2[st % 2][:, :, :], ACT.Exp)
                    else:
                        for r in range(2):
                            o = (2 * half + r) * P
                            last = act.activation(buf[:, 2 * half + r, o:], s2[st % 2][:, r, o:], ACT.Exp)
                    last.then_inc(s2_read, 1)
                    if st - 2 in ends:
                        evacuate(i, n, nth, ends.index(st - 2))
                    if i == 1 and st - 1 in ADD_AT:
                        invert(nth, ADD_AT[st - 1])
                    if st == PLACE_AT:
                        place_max((j + 2) % SETS, n + 2)
                evacuate(i, n, nth, NC - 1)
                if i == 1:
                    invert(nth, NC - 1)

            heads(act, head)
            act.wait_ge(m_in, (B * H + 2) * 48)

        @block.tensor
        def _(pe):
            pe.sem_inc(s2_mm, (SETS - 1) * N2)
            pe.sem_inc(pv_ok, NQ)
            pe.wait_ge(filled, 4)
            pe.wait_ge(ones_ok, 2)
            pe.wait_ge(loaded_pick, 16)

            def maxima(n1, j1, turn1, st, which=slice(None)):
                for at, (t, c) in list(enumerate(first[st]))[which]:
                    v = before1[st] + at
                    w = min(C, (t + 1) * P - c * C)
                    if v == 0:
                        pe.wait_ge(loaded[j1], turn1 * 32 + 32)
                        pe.wait_ge(m_rows, n1)
                    pe.wait_ge(s1_read, n1 * N1 + v + 1)
                    last = pe.matmul(s1[v % 2][:, 0:w], qt[j1][0:STACK, t * P:(t + 1) * P],
                                     kt_[j1][0:STACK, c * C:c * C + w], start=True, stop=c < t // JT)
                    if c == t // JT:
                        last = pe.matmul(s1[v % 2][:, w - P:w], k["identb"][:, :], k["mask_qk"][:, :], start=False,
                                         stop=True)
                    last.then_inc(s1_mm, 1)

            def turn_max(n1):
                pe.wait_ge(lo_ok, n1 + 1)
                pe.wait_ge(s1_read, (n1 + 1) * N1 + 2)
                hold(pe, k)
                pe.transpose(pm, mparts[:, :, :].rearrange("p a t -> p (a t)"), k["identb"][:, :]
                             ).then_inc(m_turned, 1)

            for j in range(2):
                for st in range(N2):
                    maxima(j, j, 0, st)
                turn_max(j)

            def scores(n, j, st, tiles=range(2)):
                qc, quad, half = second[st]
                pe.wait_ge(s2_read, n * N2 + st + 1)
                for r in tiles:
                    kt = quad * QUAD + 2 * half + r
                    o = (kt - qc * QUAD) * P if quad == qc else 0
                    last = pe.matmul(s2[st % 2][:, r, o:], kt_[j][:, kt * P:(kt + 1) * P],
                                     qt[j][:, qc * C + o:(qc + 1) * C], start=True, stop=quad < qc)
                    if quad == qc:
                        last = pe.matmul(s2[st % 2][:, r, o:o + P], k["identb"][:, :], k["mask_kq"][:, :],
                                         start=False, stop=True)
                if r == 1:
                    last.then_inc(s2_mm, 1)

            def values(n, i, st):
                qc, quad, _ = second[st]
                buf = prob_buffer(st)
                pe.wait_ge(s2_read, n * N2 + st + 1 + 2)
                if quad == 0 and qc == 0:
                    pe.wait_ge(v_ok, n + 1)
                if quad == 0:
                    pe.wait_ge(pv_out, n * NC + qc)
                for g in range(QUAD):
                    last = pe.matmul(pv[32 * g:32 * g + 32, :], vs[i][:, quad * QUAD + g, :], buf[:, g, :],
                                     start=quad == 0, stop=quad == qc, skip_group_check=True)
                last.then_inc(pv_ok, 1)

            def add(nth, qc):
                pe.wait_ge(pv_out, (nth * 2 + 1) * NC + qc + 1)
                pe.wait_ge(out_ok, nth * NC + qc)
                for i in range(2):
                    last = pe.matmul(px[0:64, :], pick[:, i, :], sums[i][:, qc, :], start=i == 0, stop=i == 1)
                last.then_inc(added, 1)

            def begin(n, j):
                pe.wait_ge(m_in, n * 48 + 48)
                for st in range(2):
                    scores(n, j, st)

            begin(0, 0)

            def head(b, hp, i, n, nth, j, turn):
                for st in range(N2):
                    own = len(first[st])
                    cut = (max(own - 2, 0), max(own - 2, 0)) if st % 2 == 0 else (1, 1)
                    maxima(n + 2, (j + 2) % SETS, turn + (j + 2) // SETS, st, slice(0, cut[0]))
                    if st >= 2:
                        scores(n, j, st, [0])
                    maxima(n + 2, (j + 2) % SETS, turn + (j + 2) // SETS, st, slice(cut[0], cut[1]))
                    if st >= 2:
                        scores(n, j, st, [1])
                    maxima(n + 2, (j + 2) % SETS, turn + (j + 2) // SETS, st, slice(cut[1], None))
                    if st == TURN_AT:
                        turn_max(n + 2)
                    if st % 2 == 0 and 0 < st < N2 - 2:
                        values(n, i, st - 1)
                    if i == 1 and st in ADD_AT:
                        add(nth, ADD_AT[st])
                values(n, i, N2 - 3)
                begin(n + 1, (j + 1) % SETS)
                values(n, i, N2 - 1)
                if i == 1:
                    add(nth, NC - 1)

            heads(pe, head)


def head_picks():
    import numpy as np
    pick = np.zeros((4, 32, 2, 64), np.float32)
    for i in range(2):
        for r in range(HD):
            pick[:, r, i, HD * i + r] = 1
            pick[:, HD, i, 32 + HD * i + r] = 1
    return pick.reshape(P, 2, 64)



def route(nc, k, attnT, xf, wproj, g2, b2, wgate, expert_iota, x3, exp_in, slots, gates):
    with Stage(nc, "route") as s:
        at = [s.sb(f"at{i}", [P, KD, C]) for i in range(2)]
        xt = [s.sb(f"xt{i}", [P, JT, D]) for i in range(2)]
        wp = s.sb("wp", [P, KD, D])
        wg = s.sb("wg", [P, KD, E])
        gb = s.sb("gb", [P, 2, D])
        iota = s.sb("iota", [P, E])
        tri = s.sb("tri", [P, P], BF16)
        ones = s.sb("ones", [P, P], BF16)
        x3t = s.sb("x3t", [P, JT, D])
        ht = [s.sb(f"ht{i}", [P, JT, D]) for i in range(NC)]
        hT = s.sb("hT", [P, KD, C])
        stats = s.sb("stats", [P, JT, 6])
        mv = s.sb("mv", [P, JT, 2])
        rstd = s.sb("rstd", [P, JT])
        lmax = s.sb("lmax", [P, JT])
        ex = s.sb("ex", [P, JT, E])
        den = s.sb("den", [P, JT])
        gt = s.sb("gt", [P, JT, E])
        top = s.sb("top", [P, JT, 8])
        topi = s.sb("topi", [P, JT, 8], U32)
        chosen = s.sb("chosen", [P, JT, 2])
        hot = s.sb("hot", [P, JT, 2, E])
        mask = s.sb("mask", [P, JT, E], BF16)
        base = s.sb("base", [P, E])
        rank = s.sb("rank", [P, JT, E])
        prod = s.sb("prod", [P, JT, 2, E])
        place = s.sb("place", [P, JT, 2])
        over = s.sb("over", [P, JT, 2])
        clipped = s.sb("clipped", [P, JT, 2])
        slot_f = s.sb("slot_f", [P, JT, 2])
        send = k["offsets"]
        po = s.ps("po", [P, JT, D])
        turn = [s.ps(f"turn{i}", [P, C]) for i in range(KD)]
        pg = s.ps("pg", [P, JT, E])
        pc = s.ps("pc", [P, JT + 1, E])
        loaded = s.sems("loaded0", "loaded1")
        sent = s.pool_dma_sems(*[f"sent{i}" for i in range(NC)])
        (stored_x3,) = s.sems("stored_x3")
        (loaded_w, tri0, tri_ok, base_ok, o_mm, x3_ok, st_ok, mv_ok, log_ok, rstd_ok, n_ok, h_ok,
         h_turned, h_out_a, h_out_d, g_mm, max_ok, sub_ok, ex_ok, sum_ok, rec_ok, gt_ok, top_ok, topi_ok,
         chosen_ok, hot_ok, mask_ok, c_mm, rank_ok, prod_ok, place_ok, over_ok, based, slot_ok, send_ok) = s.sems(
            "loaded_w", "tri0", "tri_ok", "base_ok", "o_mm", "x3_ok", "st_ok", "mv_ok", "log_ok",
            "rstd_ok", "n_ok", "h_ok", "h_turned", "h_out_a", "h_out_d", "g_mm", "max_ok", "sub_ok", "ex_ok",
            "sum_ok", "rec_ok", "gt_ok", "top_ok", "topi_ok", "chosen_ok", "hot_ok", "mask_ok", "c_mm", "rank_ok",
            "prod_ok", "place_ok", "over_ok", "based", "slot_ok", "send_ok")
        NW = 5
        HB = NC // 2
        atv = attnT.rearrange("b (m p) l -> b p m l", p=P)
        xfv, x3v = tok_view(xf), tok_view(x3)
        block = s.block()

        def chunks(eng, body):
            with eng.Fori(0, B) as b:
                for c in range(NC):
                    body(b, c, b * NC + c, c % 2, b * HB + c // 2, b * HB + (c + 1) // 2)

        @block.sync
        def _(sp):
            for dst, src in ((wp[:, :, :], wproj.rearrange("(k p) m -> p k m", p=P)),
                             (wg[:, :, :], wgate.rearrange("(k p) m -> p k m", p=P)),
                             (gb[:, 0, :], g2.broadcast_to([P, D])), (gb[:, 1, :], b2.broadcast_to([P, D])),
                             (iota[:, :], expert_iota.broadcast_to([P, E]))):
                sp.dma_start(dst, src).then_inc(loaded_w, 16)

            def load(b, c, t, i, nth, nth_n):
                sp.wait_ge(x3_ok, t + 1)
                sp.dma_start(at[i][:, :, :], atv[b, :, :, c * C:(c + 1) * C]).then_inc(loaded[i], 16)
                sp.dma_start(xt[i][:, :, :], xfv[b, c]).then_inc(loaded[i], 16)

            chunks(sp, load)
            for i in range(2):
                load(0, 0, B * NC + i, i, 0, 0)

        @block.gpsimd
        def _(pool):
            pool.memset(ones[:, :], 1.0).then_inc(tri0, 1)
            pool.wait_ge(tri0, 1)
            pool.affine_select(out=tri[:, :], in_=ones[:, :], compare_op=ALU.is_ge, fill=0.0, base=0,
                               pattern=[[1, P]], channel_multiplier=-1).then_inc(tri_ok, 1)

            def chunk(b, c, t, i, nth, nth_n):
                pool.wait_ge(send_ok, t + 1)
                hold(pool, k)
                for j in range(JT):
                    for w in range(2):
                        pool.indirect_dma_start(
                            out=exp_in, out_offset=bass.IndirectOffsetOnAxis(ap=send[i][:, j, w:w + 1], axis=0),
                            in_=ht[c][:, j, :], in_offset=None, bounds_check=E * CAP - 1, oob_is_err=False
                        ).then_inc(sent[c], 16)

            chunks(pool, chunk)
            for i in range(NC):
                pool.wait_ge(sent[i], 16 * B * JT * 2)

        @block.vector
        def _(dve):
            dve.wait_ge(loaded_w, 16 * NW)
            dve.memset(base[:, :], 0.0).then_inc(base_ok, 1)
            dve.sem_inc(x3_ok, 2)

            def make_x3(i, n):
                dve.wait_ge(o_mm, n + 1)
                dve.wait_ge(stored_x3, n * 16)
                dve.tensor_tensor(x3t[:, :, :], po[:, :, :], xt[i][:, :, :], ALU.add).then_inc(x3_ok, 1)
                dve.wait_ge(x3_ok, n + 3)
                for j in range(JT):
                    last = dve.bn_stats(stats[:, j, :], x3t[:, j, :])
                last.then_inc(st_ok, 1)
                dve.wait_ge(st_ok, n + 1)
                hold(dve, k)
                for j in range(JT):
                    last = dve.bn_aggr(mv[:, j, :], stats[:, j, :])
                last.then_inc(mv_ok, 1)

            def make_h(c, n, b):
                h = ht[c]
                dve.wait_ge(rstd_ok, n + 1)
                dve.wait_ge(sent[c], b * (JT * 2 * 16))
                for j in range(JT):
                    last = dve.tensor_scalar(h[:, j, :], x3t[:, j, :], mv[:, j, 0:1], rstd[:, j:j + 1],
                                             ALU.subtract, ALU.mult)
                last.then_inc(n_ok, 1)
                dve.wait_ge(n_ok, n + 1)
                dve.tensor_tensor(h[:, :, :], h[:, :, :], gb[:, 0:1, :].broadcast_to([P, JT, D]), ALU.mult
                                  ).then_inc(h_ok, 1)
                dve.wait_ge(h_ok, n * 2 + 1)
                dve.tensor_tensor(h[:, :, :], h[:, :, :], gb[:, 1:2, :].broadcast_to([P, JT, D]), ALU.add
                                  ).then_inc(h_ok, 1)

            def copy_turned(n):
                dve.wait_ge(h_turned, n * KD + 2)
                dve.tensor_copy(hT[:, 1, :], turn[1][:, :]).then_inc(h_out_d, 1)

            make_x3(0, 0)
            make_h(0, 0, 0)
            copy_turned(0)

            def chunk(b, c, t, i, nth, nth_n):
                dve.wait_ge(g_mm, t + 1)
                dve.tensor_reduce(lmax[:, :], pg[:, :, :], AX_X, ALU.max).then_inc(max_ok, 1)
                dve.wait_ge(max_ok, t + 1)
                dve.tensor_tensor(ex[:, :, :], pg[:, :, :], lmax[:, :].unsqueeze(2).broadcast_to([P, JT, E]),
                                  ALU.subtract).then_inc(sub_ok, 1)
                make_x3(1 - i, t + 1)
                dve.wait_ge(ex_ok, t + 1)
                dve.tensor_reduce(den[:, :], ex[:, :, :], AX_X, ALU.add).then_inc(sum_ok, 1)
                dve.wait_ge(sum_ok, t + 1)
                dve.reciprocal(den[:, :], den[:, :]).then_inc(rec_ok, 1)
                dve.wait_ge(rec_ok, t + 1)
                dve.tensor_tensor(gt[:, :, :], ex[:, :, :], den[:, :].unsqueeze(2).broadcast_to([P, JT, E]),
                                  ALU.mult).then_inc(gt_ok, 1)
                dve.wait_ge(gt_ok, t + 1)
                hold(dve, k)
                for j in range(JT):
                    last = dve.max(top[:, j, :], gt[:, j, :])
                last.then_inc(top_ok, 1)
                dve.wait_ge(top_ok, t + 1)
                hold(dve, k)
                for j in range(JT):
                    last = dve.max_index(topi[:, j, :], top[:, j, :], gt[:, j, :])
                last.then_inc(topi_ok, 1)
                dve.wait_ge(topi_ok, t + 1)
                dve.tensor_copy(chosen[:, :, :], topi[:, :, 0:2]).then_inc(chosen_ok, 1)
                dve.wait_ge(chosen_ok, t + 1)
                for w in range(2):
                    last = dve.tensor_tensor(hot[:, :, w, :], iota[:, :].unsqueeze(1).broadcast_to([P, JT, E]),
                                             chosen[:, :, w:w + 1].broadcast_to([P, JT, E]), ALU.is_equal)
                last.then_inc(hot_ok, 1)
                dve.wait_ge(hot_ok, t + 1)
                dve.wait_ge(c_mm, t)
                dve.tensor_tensor(mask[:, :, :], hot[:, :, 0, :], hot[:, :, 1, :], ALU.add).then_inc(mask_ok, 1)
                make_h((c + 1) % NC, t + 1, b + (c + 1) // NC)
                dve.wait_ge(c_mm, t + 1)
                dve.wait_ge(base_ok, t + 1)
                dve.tensor_tensor(rank[:, :, :], pc[:, 0:JT, :], base[:, :].unsqueeze(1).broadcast_to([P, JT, E]),
                                  ALU.add).then_inc(rank_ok, 1)
                dve.wait_ge(rank_ok, t + 1)
                dve.tensor_tensor(base[:, :], base[:, :], pc[:, JT, :], ALU.add).then_inc(base_ok, 1)
                for w in range(2):
                    last = dve.tensor_tensor(prod[:, :, w, :], hot[:, :, w, :], rank[:, :, :], ALU.mult)
                last.then_inc(prod_ok, 1)
                dve.wait_ge(prod_ok, t + 1)
                dve.tensor_reduce(place[:, :, :], prod[:, :, :, :], AX_X, ALU.add).then_inc(place_ok, 1)
                dve.wait_ge(place_ok, t + 1)
                dve.tensor_scalar(over[:, :, :], place[:, :, :], float(CAP), None, ALU.is_gt)
                dve.tensor_scalar(clipped[:, :, :], place[:, :, :], float(CAP), -1.0, ALU.min, ALU.add
                                  ).then_inc(over_ok, 1)
                dve.wait_ge(over_ok, t + 1)
                dve.scalar_tensor_tensor(out=slot_f[:, :, :], in0=chosen[:, :, :], scalar=float(CAP),
                                         in1=clipped[:, :, :], op0=ALU.mult, op1=ALU.add).then_inc(based, 1)
                dve.wait_ge(based, t + 1)
                at4 = bass.ds(t * JT, JT)
                dve.tensor_copy(slots[:, at4, :], slot_f[:, :, :]).then_inc(slot_ok, 1)
                dve.wait_ge(sent[(c + 2) % NC], (b + c // 2) * (JT * 2 * 16))
                dve.scalar_tensor_tensor(out=send[i][:, :, :], in0=over[:, :, :], scalar=BIG_SLOT,
                                         in1=slot_f[:, :, :], op0=ALU.mult, op1=ALU.add).then_inc(send_ok, 1)
                dve.tensor_scalar(clipped[:, :, :], over[:, :, :], -1.0, 1.0, ALU.mult, ALU.add
                                  ).then_inc(slot_ok, 1)
                dve.wait_ge(slot_ok, t * 3 + 2)
                dve.tensor_tensor(gates[:, at4, :], top[:, :, 0:2], clipped[:, :, :], ALU.mult).then_inc(slot_ok, 1)
                dve.wait_ge(slot_ok, t * 3 + 3)
                copy_turned(t + 1)

            chunks(dve, chunk)

        @block.scalar
        def _(act):
            act.preload_act_table_set(EXP_AND_LN)

            def serve_ln(n):
                act.wait_ge(mv_ok, n + 1)
                act.activation(rstd[:, :], mv[:, :, 1], ACT.Ln, bias=k["eps"][:, :]).then_inc(log_ok, 1)
                act.wait_ge(log_ok, n + 1)
                act.activation(rstd[:, :], rstd[:, :], ACT.Exp, scale=-0.5).then_inc(rstd_ok, 1)

            def copy_turned(n):
                act.wait_ge(h_turned, n * KD + 1)
                act.activation(hT[:, 0, :], turn[0][:, :], ACT.Copy).then_inc(h_out_a, 1)

            serve_ln(0)
            copy_turned(0)

            def chunk(b, c, t, i, nth, nth_n):
                act.wait_ge(x3_ok, t + 3)
                act.dma_start(x3v[b, c], x3t[:, :, :]).then_inc(stored_x3, 16)
                act.wait_ge(sub_ok, t + 1)
                act.activation(ex[:, :, :], ex[:, :, :], ACT.Exp).then_inc(ex_ok, 1)
                serve_ln(t + 1)
                copy_turned(t + 1)

            chunks(act, chunk)
            act.wait_ge(stored_x3, 16 * B * NC)

        @block.tensor
        def _(pe):
            pe.wait_ge(loaded_w, 16 * NW)
            pe.wait_ge(tri_ok, 1)

            def project(n, i, nth):
                pe.wait_ge(x3_ok, n + 2)
                pe.wait_ge(loaded[i], nth * 32 + 32)
                for j in range(JT):
                    for m in range(KD):
                        last = pe.matmul(po[:, j, :], at[i][:, m, j * P:(j + 1) * P], wp[:, m, :], start=m == 0,
                                         stop=m == KD - 1)
                last.then_inc(o_mm, 1)

            def turn_h(n, c):
                pe.wait_ge(h_ok, n * 2 + 2)
                for m in range(KD):
                    for j in range(JT):
                        last = pe.transpose(turn[m][:, j * P:(j + 1) * P], ht[c][:, j, m * P:(m + 1) * P],
                                            k["ident"][:, :])
                    last.then_inc(h_turned, 1)

            def logits(n):
                pe.wait_ge(h_out_a, n + 1)
                pe.wait_ge(h_out_d, n + 1)
                pe.wait_ge(sub_ok, n)
                for j in range(JT):
                    for m in range(KD):
                        last = pe.matmul(pg[:, j, :], hT[:, m, j * P:(j + 1) * P], wg[:, m, :], start=m == 0,
                                         stop=m == KD - 1)
                last.then_inc(g_mm, 1)

            project(0, 0, 0)
            project(1, 1, 0)
            turn_h(0, 0)
            logits(0)

            def chunk(b, c, t, i, nth, nth_n):
                pe.wait_ge(mask_ok, t + 1)
                pe.wait_ge(base_ok, t + 1)
                for j in range(JT + 1):
                    for j2 in range(min(j, JT - 1) + 1):
                        last = pe.matmul(pc[:, j, :], (tri if j2 == j else ones)[:, :], mask[:, j2, :],
                                         start=j2 == 0, stop=j2 == min(j, JT - 1))
                last.then_inc(c_mm, 1)
                project(t + 2, i, nth + 1)
                turn_h(t + 1, (c + 1) % NC)
                logits(t + 1)

            chunks(pe, chunk)



def run_experts(nc, k, exp_in, w1, b1, w2, b2, exp_out):
    ST = CAP // P
    CH = CAP // C
    FT = FF // P
    with Stage(nc, "experts") as s:
        xt = [s.sb(f"xt{i}", [P, ST, D]) for i in range(2)]
        w1t = [s.sb(f"w1t{i}", [P, KD, FF]) for i in range(2)]
        w2t = [s.sb(f"w2t{i}", [P, FT, D]) for i in range(2)]
        b1t = [s.sb(f"b1t{i}", [P, FT]) for i in range(2)]
        b2t = [s.sb(f"b2t{i}", [P, D]) for i in range(2)]
        xT = s.sb("xT", [P, KD, CAP])
        hid = [s.sb(f"hid{i}", [P, FT, C]) for i in range(CH)]
        yt = [s.sb(f"yt{i}", [P, JT, D]) for i in range(CH)]
        turn = [s.ps(f"turn{i}", [P, C]) for i in range(KD * CH)]
        ph = [s.ps(f"ph{i}", [P, C]) for i in range(2)]
        py = [s.ps(f"py{i}", [P, D]) for i in range(2)]
        loaded = s.sems("loaded0", "loaded1")
        stored = s.pool_dma_sems("stored0", "stored1")
        (turned, x_out, h_mm, h_ok, y_mm, y_ok) = s.sems("turned", "x_out", "h_mm", "h_ok", "y_mm", "y_ok")
        NL = 5
        xv = exp_in.rearrange("(e t p) d -> e p t d", e=E, p=P)
        yv = exp_out.rearrange("(e c t p) d -> e c p t d", e=E, c=CH, p=P)
        block = s.block()
        NH = CH * FT

        def experts(eng, body):
            with eng.Fori(0, E // 2) as pair:
                for i in range(2):
                    body(pair * 2 + i, i, pair)

        @block.sync
        def _(sp):
            def load(e, i, nth):
                sp.wait_ge(y_ok, e * ST)
                for dst, src in ((xt[i][:, :, :], xv[e]), (w1t[i][:, :, :], w1[e].rearrange("(k p) f -> p k f", p=P)),
                                 (b1t[i][:, :], b1[e].rearrange("p f -> p f")),
                                 (w2t[i][:, :, :], w2[e].rearrange("(f p) d -> p f d", p=P)),
                                 (b2t[i][:, :], b2[bass.ds(e, 1), :].broadcast_to([P, D]))):
                    sp.dma_start(dst, src).then_inc(loaded[i], 16)

            experts(sp, load)

        @block.gpsimd
        def _(pool):
            def store(e, i, nth):
                for ch in range(CH):
                    pool.wait_ge(y_ok, (e + 1) * ST + (ch + 1) * JT)
                    hold(pool, k)
                    pool.dma_start(yv[e, ch], yt[ch][:, :, :]).then_inc(stored[ch], 16)

            experts(pool, store)
            for ch in range(CH):
                pool.wait_ge(stored[ch], 16 * E)

        @block.vector
        def _(dve):
            dve.sem_inc(y_ok, ST)

            def body(e, i, nth):
                for q in range(KD * CH):
                    dve.wait_ge(turned, e * (KD * CH) + q + 1)
                    dve.wait_ge(h_mm, e * NH)
                    m, ch = q // CH, q % CH
                    dve.tensor_copy(xT[:, m, ch * C:(ch + 1) * C], turn[q][:, :]).then_inc(x_out, 1)
                for j in range(ST):
                    if j % JT == 0:
                        dve.wait_ge(stored[j // JT], e * 16)
                    dve.wait_ge(y_mm, e * ST + j + 1)
                    dve.tensor_tensor(yt[j // JT][:, j % JT, :], py[j % 2][:, :], b2t[i][:, :], ALU.add
                                      ).then_inc(y_ok, 1)

            experts(dve, body)

        @block.scalar
        def _(act):
            def body(e, i, nth):
                act.wait_ge(loaded[i], nth * (16 * NL) + 16 * NL)
                for q in range(NH):
                    ch, f = q // FT, q % FT
                    act.wait_ge(h_mm, e * NH + q + 1)
                    act.wait_ge(y_mm, e * ST)
                    act.activation(hid[ch][:, f, :], ph[q % 2][:, :], ACT.Gelu, bias=b1t[i][:, f:f + 1]
                                   ).then_inc(h_ok, 1)

            experts(act, body)

        @block.tensor
        def _(pe):
            def body(e, i, nth):
                pe.wait_ge(loaded[i], nth * (16 * NL) + 16 * NL)
                for q in range(KD * CH):
                    m, ch = q // CH, q % CH
                    for j in range(JT):
                        t = ch * JT + j
                        last = pe.transpose(turn[q][:, j * P:(j + 1) * P], xt[i][:, t, m * P:(m + 1) * P],
                                            k["ident"][:, :])
                    last.then_inc(turned, 1)
                pe.wait_ge(x_out, (e + 1) * (KD * CH))
                for q in range(NH):
                    ch, f = q // FT, q % FT
                    if q < 2:
                        pe.wait_ge(h_ok, e * NH)
                    else:
                        pe.wait_ge(h_ok, e * NH + q - 1)
                    for m in range(KD):
                        last = pe.matmul(ph[q % 2][:, :], w1t[i][:, m, f * P:(f + 1) * P],
                                         xT[:, m, ch * C:(ch + 1) * C], start=m == 0, stop=m == KD - 1)
                    last.then_inc(h_mm, 1)
                for j in range(ST):
                    ch = j // JT
                    pe.wait_ge(h_ok, e * NH + (ch + 1) * FT)
                    pe.wait_ge(y_ok, (e + 1) * ST + j - 1)
                    for f in range(FT):
                        last = pe.matmul(py[j % 2][:, :], hid[ch][:, f, (j % JT) * P:(j % JT + 1) * P],
                                         w2t[i][:, f, :], start=f == 0, stop=f == FT - 1)
                    last.then_inc(y_mm, 1)

            experts(pe, body)



def combine(nc, k, exp_out, slots, gates, x3, x1, out):
    with Stage(nc, "combine") as s:
        idx = k["offsets"]
        gt = [s.sb(f"gt{i}", [P, JT, 2]) for i in range(2)]
        rows = [s.sb(f"rows{i}", [P, JT, 2, D]) for i in range(2)]
        x3t = [s.sb(f"x3t{i}", [P, JT, D]) for i in range(2)]
        x1t = [s.sb(f"x1t{i}", [P, JT, D]) for i in range(2)]
        ot = [s.sb(f"ot{i}", [P, JT, D]) for i in range(2)]
        stats = s.sb("stats", [P, JT, 6])
        mv = s.sb("mv", [P, JT, 2])
        rstd = s.sb("rstd", [P, JT])
        loaded = s.sems("loaded0", "loaded1")
        fetched = s.pool_dma_sems("fetched0", "fetched1")
        stored = s.sems("stored0", "stored1")
        (idx_ok, one_ok, two_ok, st_ok, mv_ok, log_ok, rstd_ok, n_ok, out_ok) = s.sems(
            "idx_ok", "one_ok", "two_ok", "st_ok", "mv_ok", "log_ok", "rstd_ok", "n_ok", "out_ok")
        HB = NC // 2
        x3v, x1v, ov = tok_view(x3), tok_view(x1), tok_view(out)
        block = s.block()

        def chunks(eng, body):
            with eng.Fori(0, B) as b:
                for c in range(NC):
                    body(b, c, b * NC + c, c % 2, b * HB + c // 2)

        @block.sync
        def _(sp):
            def load(b, c, t, i, nth):
                sp.wait_ge(out_ok, t + 1)
                sp.dma_start(x3t[i][:, :, :], x3v[b, c]).then_inc(loaded[i], 16)
                sp.dma_start(x1t[i][:, :, :], x1v[b, c]).then_inc(loaded[i], 16)

            chunks(sp, load)

        @block.gpsimd
        def _(pool):
            def fetch(b, c, t, i, nth):
                pool.wait_ge(two_ok, t + 1)
                at4 = bass.ds(t * JT, JT)
                pool.tensor_copy(idx[i][:, :, :], slots[:, at4, :]).then_inc(idx_ok, 1)
                pool.tensor_copy(gt[i][:, :, :], gates[:, at4, :]).then_inc(idx_ok, 1)
                pool.wait_ge(idx_ok, t * 2 + 2)
                hold(pool, k)
                for j in range(JT):
                    for w in range(2):
                        pool.indirect_dma_start(
                            out=rows[i][:, j, w, :], out_offset=None, in_=exp_out,
                            in_offset=bass.IndirectOffsetOnAxis(ap=idx[i][:, j, w:w + 1], axis=0),
                            bounds_check=E * CAP - 1, oob_is_err=False).then_inc(fetched[i], 16)

            chunks(pool, fetch)

        @block.vector
        def _(dve):
            dve.sem_inc(out_ok, 2)
            dve.sem_inc(two_ok, 2)

            def chunk(b, c, t, i, nth):
                dve.wait_ge(loaded[i], nth * 32 + 32)
                dve.wait_ge(fetched[i], nth * (JT * 2 * 16) + JT * 2 * 16)
                dve.wait_ge(stored[i], nth * 16)
                for j in range(JT):
                    last = dve.scalar_tensor_tensor(out=x3t[i][:, j, :], in0=rows[i][:, j, 0, :],
                                                    scalar=gt[i][:, j, 0:1], in1=x3t[i][:, j, :], op0=ALU.mult,
                                                    op1=ALU.add)
                last.then_inc(one_ok, 1)
                dve.wait_ge(one_ok, t + 1)
                for j in range(JT):
                    last = dve.scalar_tensor_tensor(out=ot[i][:, j, :], in0=rows[i][:, j, 1, :],
                                                    scalar=gt[i][:, j, 1:2], in1=x3t[i][:, j, :], op0=ALU.mult,
                                                    op1=ALU.add)
                last.then_inc(two_ok, 1)
                dve.wait_ge(two_ok, t + 3)
                for j in range(JT):
                    last = dve.bn_stats(stats[:, j, :], ot[i][:, j, :])
                last.then_inc(st_ok, 1)
                dve.wait_ge(st_ok, t + 1)
                hold(dve, k)
                for j in range(JT):
                    last = dve.bn_aggr(mv[:, j, :], stats[:, j, :])
                last.then_inc(mv_ok, 1)
                dve.wait_ge(rstd_ok, t + 1)
                for j in range(JT):
                    last = dve.tensor_scalar(ot[i][:, j, :], ot[i][:, j, :], mv[:, j, 0:1], rstd[:, j:j + 1],
                                             ALU.subtract, ALU.mult)
                last.then_inc(n_ok, 1)
                dve.wait_ge(n_ok, t + 1)
                dve.tensor_tensor(ot[i][:, :, :], ot[i][:, :, :], x1t[i][:, :, :], ALU.add).then_inc(out_ok, 1)

            chunks(dve, chunk)

        @block.scalar
        def _(act):
            def chunk(b, c, t, i, nth):
                act.wait_ge(mv_ok, t + 1)
                act.activation(rstd[:, :], mv[:, :, 1], ACT.Ln, bias=k["eps"][:, :]).then_inc(log_ok, 1)
                act.wait_ge(log_ok, t + 1)
                act.activation(rstd[:, :], rstd[:, :], ACT.Exp, scale=-0.5).then_inc(rstd_ok, 1)
                act.wait_ge(out_ok, t + 3)
                act.dma_start(ov[b, c], ot[i][:, :, :]).then_inc(stored[i], 16)

            act.preload_act_table_set(EXP_AND_LN)
            chunks(act, chunk)
            for i in range(2):
                act.wait_ge(stored[i], 16 * B * HB)



def sandwich_block(nc, a, out):
    def scratch(name, shape, dt=F32):
        return nc.dram_tensor(f"scratch_{name}", shape, dt, kind="Internal").ap()

    xin = scratch("xin", (B, DI, L + 2 * HALO))
    sz = scratch("sz", (NTOK, DI))
    y = scratch("y", (2 * B * NC + 1, P, JT, DI))
    x1 = scratch("x1", (NTOK, D))
    xf = scratch("xf", (NTOK, D))
    qk = scratch("qk", (B, H, 2, STACK, L), BF16)
    va = scratch("va", (NTOK, H * (HD + 1)))
    attnT = scratch("attnT", (B, D, L))
    x3 = scratch("x3", (NTOK, D))
    exp_in = scratch("exp_in", (E * CAP, D))
    exp_out = scratch("exp_out", (E * CAP, D))
    with Stage(nc, "kept") as kept:
        k = make_constants(nc, kept)
        slots = kept.sb("slots", [P, NTOK // P, 2], I32)
        gates = kept.sb("gates", [P, NTOK // P, 2])
        project_inputs(nc, k, a["u"], a["in_wT"], xin, sz, exp_in)
        scan_channels(nc, k, xin, y, a["convw"], a["convb"], a["xpw_dt"], a["xpw_bc"], a["dtw"], a["dtb"],
                      a["alog"], a["dskip"])
        mix_and_qkv(nc, k, y, sz, a["u"], a["out_wT"], a["g1"], a["b1ln"], a["wqkv"], a["rope"], x1, xf, qk, va)
        attend(nc, k, qk, va, a["pick_heads"], attnT)
        route(nc, k, attnT, xf, a["wproj"], a["g2"], a["b2ln"], a["wgate"], a["expert_iota"], x3, exp_in, slots,
              gates)
        run_experts(nc, k, exp_in, a["w1"], a["b1"], a["w2"], a["b2"], exp_out)
        combine(nc, k, exp_out, slots, gates, x3, x1, out)


def layouts(i):
    import numpy as np

    def row(a):
        return np.ascontiguousarray(np.asarray(a).reshape(1, -1))

    return {
        "u": np.ascontiguousarray(np.asarray(i["u"]).reshape(NTOK, D)),
        "in_wT": np.ascontiguousarray(np.asarray(i["in_proj_w"]).T),
        **scan_layouts(i),
        "out_wT": np.ascontiguousarray(np.asarray(i["out_proj_w"]).T),
        "g1": row(i["ln1_g"]), "b1ln": row(i["ln1_b"]),
        "wqkv": qkv_layout(i["Wqkv"]), "rope": rope_tables(), "pick_heads": head_picks(),
        "wproj": np.asarray(i["Wproj"]), "g2": row(i["ln2_g"]), "b2ln": row(i["ln2_b"]),
        "wgate": np.asarray(i["Wgate"]), "expert_iota": np.arange(E, dtype=np.float32).reshape(1, E),
        "w1": np.asarray(i["W1"]),
        "b1": np.ascontiguousarray(np.asarray(i["b1"]).reshape(E, FF // P, P).transpose(0, 2, 1)),
        "w2": np.asarray(i["W2"]), "b2": np.asarray(i["b2"]),
    }


def kernel(**inputs):
    import numpy as np
    import concourse.bacc as bacc
    from concourse.bass_utils import run_bass_kernel_spmd

    arrays = layouts({n.replace("L0_attn_", "").replace("L0_ffn_", ""): v for n, v in inputs.items()})
    nc = bacc.Bacc("TRN2", target_bir_lowering=False, num_devices=1)
    aps = {n: nc.dram_tensor(f"in_{n}", v.shape, mybir.dt.from_np(v.dtype), kind="ExternalInput").ap()
           for n, v in arrays.items()}
    out = nc.dram_tensor("out_0_dram", (NTOK, D), F32, kind="ExternalOutput").ap()
    sandwich_block(nc, aps, out)
    r = run_bass_kernel_spmd(nc, [{f"in_{n}": v for n, v in arrays.items()}], core_ids=[0])
    return np.asarray(r.results[0]["out_0_dram"]).reshape(B, L, D)
```
